# Optimizing a Trainium2 kernel written in Bass

```python
import numpy as np
import jax
import jax.numpy as jnp

def _softmax(x, axis=-1):
    return jax.nn.softmax(x, axis=axis)

def _gelu(x):
    return jax.nn.gelu(x, approximate=True)

def _silu(x):
    return jax.nn.silu(x)

def _sigmoid(x):
    return jax.nn.sigmoid(x)

def _layernorm(x, axis=-1, eps=1e-05):
    m = jnp.mean(x, axis=axis, keepdims=True)
    v = jnp.var(x, axis=axis, keepdims=True)
    return (x - m) / jnp.sqrt(v + eps)

def _scatter_add(tgt, idx, src, axis=0):
    return tgt.at[idx].add(src)

def _segment_sum(src, seg, n):
    return jax.ops.segment_sum(src, seg, n)
kernel_name = 'mk_gnn_resnorm_d1_gnn_r64_036fb8'

def setup_inputs(seed: int=0):
    np.random.seed(seed)
    _w = jnp.asarray

    def _rec_inputs():
        import jax
        import jax.numpy as jnp
        _gk = jax.random.key(seed)
        x = -0.0002117 + 1 * jax.random.normal(jax.random.fold_in(_gk, 1), (50000, 512), jnp.float32)
        _s = jax.random.randint(jax.random.fold_in(_gk, 2), (6250,), 0, 50000, jnp.int32)
        _d = jax.random.randint(jax.random.fold_in(_gk, 3), (6250,), 0, 50000, jnp.int32)
        _loop = jnp.arange(50000, dtype=jnp.int32)
        src = jnp.concatenate([_s, _d, _loop])
        dst = jnp.concatenate([_d, _s, _loop])
        _o = jnp.argsort(dst, stable=True)
        src = src[_o]
        dst = dst[_o]
        return (x, src, dst)
    x, src, dst = _rec_inputs()

    def _L0_gnn_setup():
        import jax, jax.numpy as jnp
        import numpy as np
        N_NODES = 50000
        N_EDGES = 1500000
        D = 512
        LN_EPS = 1e-05

        def _layer_norm(x, gamma, beta):
            mu = jnp.mean(x, axis=-1, keepdims=True)
            var = jnp.mean(jnp.square(x - mu), axis=-1, keepdims=True)
            return (x - mu) * jax.lax.rsqrt(var + LN_EPS) * gamma + beta
        key = jax.random.key(seed)
        ks = jax.random.split(key, 8)
        scale = 1.0 / np.sqrt(D)
        return {'node_feature': jax.random.normal(ks[0], (N_NODES, D), dtype=jnp.float32), 'edge_index': jax.random.randint(ks[1], (2, N_EDGES), 0, N_NODES, dtype=jnp.int32), 'W_l': jax.random.uniform(ks[2], (D, D), jnp.float32, -scale, scale), 'b_l': jnp.zeros((D,), jnp.float32), 'W_r': jax.random.uniform(ks[3], (D, D), jnp.float32, -scale, scale), 'gamma': jnp.ones((D,), jnp.float32), 'beta': jnp.zeros((D,), jnp.float32)}
    _L0_gnn_all = _L0_gnn_setup()
    _L0_gnn_in = {k: v for k, v in _L0_gnn_all.items() if k in ('W_l', 'b_l', 'W_r', 'gamma', 'beta')}
    del _L0_gnn_all
    return {'x': x, 'src': src, 'dst': dst, 'L0_gnn_W_l': _L0_gnn_in['W_l'], 'L0_gnn_b_l': _L0_gnn_in['b_l'], 'L0_gnn_W_r': _L0_gnn_in['W_r'], 'L0_gnn_gamma': _L0_gnn_in['gamma'], 'L0_gnn_beta': _L0_gnn_in['beta']}

def reference(x, src, dst, L0_gnn_W_l, L0_gnn_b_l, L0_gnn_W_r, L0_gnn_gamma, L0_gnn_beta):
    import jax
    import jax.numpy as jnp

    def _L0_gnn_ref(node_feature, edge_index, W_l, b_l, W_r, gamma, beta):
        import jax, jax.numpy as jnp
        import numpy as np
        N_NODES = 50000
        N_EDGES = 1500000
        D = 512
        LN_EPS = 1e-05

        def _layer_norm(x, gamma, beta):
            mu = jnp.mean(x, axis=-1, keepdims=True)
            var = jnp.mean(jnp.square(x - mu), axis=-1, keepdims=True)
            return (x - mu) * jax.lax.rsqrt(var + LN_EPS) * gamma + beta
        n = node_feature.shape[0]
        residual = node_feature
        h = _layer_norm(node_feature, gamma, beta)
        src, dst = (edge_index[0], edge_index[1])
        summed = jax.ops.segment_sum(h[src], dst, num_segments=n)
        cnt = jax.ops.segment_sum(jnp.ones((src.shape[0],), h.dtype), dst, num_segments=n)
        mean = summed / jnp.maximum(cnt, 1.0)[:, None]
        out = mean @ W_l.T + b_l + h @ W_r.T
        out = jax.nn.relu(out)
        return out + residual
    edge_index = jnp.stack([src, dst])
    x = _layernorm(x + _L0_gnn_ref(x, edge_index, L0_gnn_W_l, L0_gnn_b_l, L0_gnn_W_r, L0_gnn_gamma, L0_gnn_beta), axis=-1)
    return x

_drawn_inputs = setup_inputs


def setup_inputs(seed=0):
    import zlib

    import numpy as np

    out = dict(_drawn_inputs(seed))
    spreads = {'L0_gnn_b_l': (0.0, 0.1), 'L0_gnn_gamma': (1.0, 0.2), 'L0_gnn_beta': (0.0, 0.28)}
    factors = {}
    for name, (base, spread) in spreads.items():
        noise = np.random.default_rng([zlib.crc32(name.encode()), seed]).standard_normal(out[name].shape)
        drawn = base * np.exp(spread * noise) if base else spread * noise
        out[name] = jnp.asarray(drawn.astype(out[name].dtype))
    for name, factor in factors.items():
        out[name] = (out[name] * factor).astype(out[name].dtype)
    return out
```

```python
import concourse.bass as bass
from concourse import mybir
from contextlib import ExitStack

LANES = 128
PAIR = 2
UNROLL = 4
WINDOW = 128
STRIDE = 120
RUN = WINDOW - STRIDE + 1
FAR = 1 << 20


class Step:

    def __init__(self, at, total, reg=None):
        self.at, self.total, self.reg = at, total, reg

    def plus(self, k):
        return Step(self.at + k, self.total, self.reg)

    def exists(self):
        return self.reg is not None or 0 <= self.at < self.total

    def times(self, m, k):
        if self.reg is None:
            return m * self.at + k
        return self.reg * (m * UNROLL) + (m * self.at + k)

    def slot(self, n):
        return self.at % n

    def turn(self, n, m=1, k=0):
        if self.reg is None:
            return m * (self.at // n) + k
        return self.reg * (m * (UNROLL // n)) + (m * (self.at // n) + k)


def run_steps(eng, total, ahead, body):
    first, last = UNROLL, total - ahead - 1
    loops = (last - first) // UNROLL
    for at in range(-ahead, first):
        body(Step(at, total))
    if loops > 0:
        with eng.Fori(0, loops) as reg:
            for u in range(UNROLL):
                body(Step(first + u, total, reg))
    for at in range(first + UNROLL * max(loops, 0), total + 1):
        body(Step(at, total))


def gnn_kernel(nc, x, src, dst, w_l, b_l, w_r, gamma, beta, out):
    f32, f32r, i32 = mybir.dt.float32, mybir.dt.float32r, mybir.dt.int32
    ALU, ACT, AX = mybir.AluOpType, mybir.ActivationFunctionType, mybir.AxisListType
    N, D = x.shape
    E = src.shape[0]
    KC = D // LANES
    EPS = 1e-5
    GROUP = PAIR * LANES
    NG = -(-N // GROUP)
    P = max(p for p in range(1, LANES + 1) if E % p == 0)
    C = E // P
    MORE = max(E - N, 0)
    NA = max(-(-MORE // (PAIR * STRIDE)), 1)
    ROWS = NA * PAIR * STRIDE + WINDOW
    BODIES = NG // UNROLL
    PER_BODY = -(-C // BODIES)
    QUOTA = [PER_BODY * (u + 1) // UNROLL - PER_BODY * u // UNROLL for u in range(UNROLL)]
    CPAD = PER_BODY * -(-NG // UNROLL)
    SUMW = D + 4
    NT = -(-N // LANES)
    SROWS = LANES * -(-(N + LANES) // LANES)

    dense = nc.dram_tensor("dense_edges", (ROWS, 3), i32, kind="Internal").ap()
    table = nc.dram_tensor("sum_table", (SROWS, SUMW), f32, kind="Internal").ap()

    ctx = ExitStack()
    with ctx:
        def sb(name, shape, dt=f32):
            return ctx.enter_context(nc.sbuf_tensor(name, shape, dt))

        def sem(name):
            return ctx.enter_context(nc.semaphore(name))

        wl_hi, wl_lo = sb("wl_hi", [LANES, KC, D], f32r), sb("wl_lo", [LANES, KC, D], f32r)
        wr_hi, wr_lo = sb("wr_hi", [LANES, KC, D], f32r), sb("wr_lo", [LANES, KC, D], f32r)
        ws_hi, ws_lo = sb("ws_hi", [LANES, KC, D], f32r), sb("ws_lo", [LANES, KC, D], f32r)
        bias_l, bias_r, bias_s = sb("bias_l", [LANES, D]), sb("bias_r", [LANES, D]), sb("bias_s", [LANES, D])
        ident, ones = sb("ident", [LANES, LANES]), sb("ones", [LANES, LANES])
        eps1, eps4 = sb("eps1", [LANES, 1]), sb("eps4", [LANES, 1])
        X = sb("x_rows", [LANES, 4, PAIR, D])
        G = sb("src_rows", [LANES, 2, PAIR, D])
        ZX = sb("z_rows", [LANES, 2, PAIR, D])
        ZG = sb("z_src", [LANES, 2, PAIR, D])
        XT = sb("z_T", [LANES, 2, PAIR, D])
        ST = sb("sum_T", [LANES, 2, PAIR, D])
        XH, XL = sb("z_T_hi", [LANES, 2, PAIR, D], f32r), sb("z_T_lo", [LANES, 2, PAIR, D], f32r)
        SH, SL = sb("sum_T_hi", [LANES, 2, PAIR, D], f32r), sb("sum_T_lo", [LANES, 2, PAIR, D], f32r)
        Y = sb("y_rows", [LANES, 2, PAIR, D])
        O = sb("out_rows", [LANES, 2, PAIR, D])
        SEL = sb("same_dst", [LANES, 2, PAIR, LANES])
        DB = sb("dst_wide", [LANES, 2, PAIR, LANES])

        def stats(name):
            return (sb(name + "_bn", [LANES, 2, PAIR, 6]), sb(name + "_mv", [LANES, 2, PAIR, 2]),
                    sb(name + "_sd", [LANES, 2, PAIR]), sb(name + "_rs", [LANES, 2, PAIR]),
                    sb(name + "_nm", [LANES, 2, PAIR]))

        xs, gs, ys = stats("xst"), stats("gst"), stats("yst")
        IDX = sb("edge_idx", [LANES, 4, PAIR, 3], i32)
        NID = sb("node_idx", [LANES, 4, PAIR], i32)
        DCF = sb("dst_f", [LANES, 4, PAIR])
        CNT, RC = sb("count", [LANES, 4, PAIR]), sb("rcount", [LANES, 4, PAIR])
        slot_far = sb("slot_far", [LANES, PAIR])
        lane_no = sb("lane_no", [LANES, 1])
        earlier = sb("earlier", [LANES, LANES])
        e_d, e_s = sb("e_dst", [P, C], i32), sb("e_src", [P, C], i32)
        e_next, e_prev = sb("e_next", [P, C], i32), sb("e_prev", [P, C], i32)
        e_run, e_no = sb("e_run", [P, C], i32), sb("e_no", [P, C], i32)
        f_a, f_b, f_v = sb("f_a", [P, C]), sb("f_b", [P, C]), sb("f_v", [P, C])
        f_nl = sb("f_nl", [P, C])
        v_sum = sb("v_sum", [P, 1])
        flag = sb("flag", [1, 1], i32)
        REC = sb("records", [P, CPAD, 4], i32)
        STG = sb("rec_stage", [P, UNROLL, max(QUOTA), 4], i32)
        tail_rec = sb("tail_rec", [1, (ROWS - MORE) * 3], i32)
        gcol, bcol = sb("gamma_col", [LANES, KC]), sb("beta_col", [LANES, KC])
        blrow = sb("bl_row", [1, D])
        S2 = sb("sum_rows", [LANES, SUMW])
        bwide = ST[:, 1, :, :].rearrange("p t (k c) -> p (t k) c", c=LANES)

        PT = [ctx.enter_context(nc.psum_tensor(f"pT{t}", [LANES, D], f32)) for t in range(PAIR)]
        PS = [ctx.enter_context(nc.psum_tensor(f"pS{t}", [LANES, D], f32)) for t in range(PAIR)]
        PL = [ctx.enter_context(nc.psum_tensor(f"pL{t}", [LANES, D], f32)) for t in range(PAIR)]
        PR = [ctx.enter_context(nc.psum_tensor(f"pR{t}", [LANES, D], f32)) for t in range(PAIR)]
        PZ = [PL, PR]

        s_w, s_edges, s_small = sem("weights_in"), sem("edges_in"), sem("small_in")
        s_pad, s_id0, s_const = sem("edge_pads_set"), sem("ident_zeroed"), sem("constants_set")
        s_wT, s_wdone, s_bias, s_setup = sem("weights_T"), sem("weights_split"), sem("bias_psum"), sem("setup_done")
        s_chain, s_viol, s_flagp, s_flag = sem("dve_setup_chain"), sem("violations"), sem("flag_psum"), sem("flag_set")
        s_passed = sem("waits_passed")
        s_tail, s_pool0 = sem("tail_written"), sem("pool_setup_chain")
        b_ld = [sem(f"b_x_in{i}") for i in range(4)]
        b_st = [sem(f"b_out_stored{i}") for i in range(2)]
        b_bn, b_var, b_sd, b_rs, b_nm = (sem("b_x_" + n) for n in ("bn", "var", "sd", "rs", "nm"))
        b_zn, b_T, b_xt, b_hi, b_lo, b_z = (sem("b_" + n) for n in ("z_rows", "z_T_psum", "z_T", "hi", "lo", "product"))
        b_t, b_y, b_ybn, b_yvar, b_ysd, b_yrs, b_ynm, b_out = (
            sem("b_" + n) for n in ("biased", "y", "y_bn", "y_var", "y_sd", "y_rs", "y_nm", "out"))
        b_stage = sem("b_records_staged")
        b_sc = [sem(f"b_scattered{i}") for i in range(UNROLL)]
        a_idx = [sem(f"a_idx_in{i}") for i in range(4)]
        a_gx = [sem(f"a_x_gathered{i}") for i in range(4)]
        a_gg = [sem(f"a_src_gathered{i}") for i in range(4)]
        a_st = [sem(f"a_out_scattered{i}") for i in range(2)]
        a_bn, a_var, a_sd, a_rs, a_nm = (sem("a_in_" + n) for n in ("bn", "var", "sd", "rs", "nm"))
        a_prep, a_D, a_sel, a_cnt, a_cnt1, a_rc = (
            sem("a_" + n) for n in ("dst_ready", "dst_psum", "same_dst", "cnt", "cnt1", "rcount"))
        a_zx, a_zg, a_T, a_S, a_xt, a_hi, a_lo = (
            sem("a_" + n) for n in ("z_rows", "z_src", "z_T_psum", "sum_psum", "z_T", "hi", "lo"))
        a_sT, a_sh, a_sl, a_z = (sem("a_" + n) for n in ("sum_T", "sum_hi", "sum_lo", "products"))
        a_t1, a_t2, a_y, a_ybn, a_yvar, a_ysd, a_yrs, a_ynm, a_out = (
            sem("a_" + n) for n in ("left", "both", "y", "y_bn", "y_var", "y_sd", "y_rs", "y_nm", "out"))
        g_zero, g_ld, g_gat, g_add = sem("g_zeroed"), sem("g_edges_in"), sem("g_gathered"), sem("g_added")
        g_dve, g_act, g_pe = sem("g_dve"), sem("g_act"), sem("g_pe")
        g_in, g_st = sem("g_rows_in"), sem("g_stored")

        block = ctx.enter_context(nc.Block())

        def wide(ap, n):
            return ap.to_broadcast([ap.shape[0], n])

        def node_rows(dram, s):
            if s.reg is None:
                base = min(s.at * GROUP, N - GROUP)
                rows = dram[base:base + GROUP, :]
            else:
                rows = dram[bass.ds(s.times(GROUP, 0), GROUP), :]
            return rows.rearrange("(p t) d -> p t d", t=PAIR)

        def windows(s):
            def one(t):
                if s.reg is None:
                    b = s.at * PAIR * STRIDE + t * STRIDE
                    return dense[b:b + WINDOW, :]
                return dense[bass.ds(s.times(PAIR * STRIDE, t * STRIDE), WINDOW), :]
            return [one(t) for t in range(PAIR)]

        def b_done(eng):
            for i in range(2):
                eng.wait_ge(b_st[i], 16 * len(range(i, NG, 2)))

        def wait_alone(eng, semaphore, value):
            eng.wait_ge(semaphore, value)
            eng.sem_inc(s_passed, 1)

        def when_fast(eng, fast, general):
            eng.wait_ge(s_flag, 1)
            bad = eng.value_load(flag[0:1, 0:1], min_val=0, max_val=4 * E)
            with eng.If(bad == 0):
                fast()
            with eng.Else():
                general()

        EDGE_DVE, EDGE_ACT, EDGE_PE = 17, 2, 2
        T_DVE, T_ACT, T_PE = 16, 5, 2

        def CHUNK_DVE(k, n):
            return k * EDGE_DVE + n

        def CHUNK_ACT(k, n):
            return k * EDGE_ACT + n

        def CHUNK_PE(k, n):
            return k * EDGE_PE + n

        def TILE_DVE(i, n):
            return i * T_DVE + (C * EDGE_DVE + n)

        def TILE_ACT(i, n):
            return i * T_ACT + (C * EDGE_ACT + n)

        def TILE_PE(i, n):
            return i * T_PE + (C * EDGE_PE + n)

        @block.sync
        def _(sp):
            sp.dma_start(G[:, :, :, :].rearrange("p a b d -> p (a b) d"),
                         w_l.rearrange("(k p) i -> p k i", p=LANES)).then_inc(s_w, 16)
            sp.dma_start(ZG[:, :, :, :].rearrange("p a b d -> p (a b) d"),
                         w_r.rearrange("(k p) i -> p k i", p=LANES)).then_inc(s_w, 16)
            sp.dma_start(gcol[:, :], gamma.rearrange("(k p) -> p k", p=LANES),
                         allow_slow_non_contiguous=True).then_inc(s_small, 16)
            sp.dma_start(bcol[:, :], beta.rearrange("(k p) -> p k", p=LANES),
                         allow_slow_non_contiguous=True).then_inc(s_small, 16)
            sp.dma_start(blrow[0:1, :], b_l.rearrange("(a d) -> a d", a=1)).then_inc(s_small, 16)
            sp.dma_start(e_d[:, :], dst.rearrange("(p c) -> p c", c=C)).then_inc(s_edges, 16)
            sp.dma_start(e_s[:, :], src.rearrange("(p c) -> p c", c=C)).then_inc(s_edges, 16)
            sp.wait_ge(s_pad, 1)
            for shifted, k in ((e_next, 1), (e_run, RUN + 1)):
                sp.dma_start(shifted[0:P - 1, :],
                             dst[k:k + (P - 1) * C].rearrange("(p c) -> p c", c=C)).then_inc(s_edges, 16)
                sp.dma_start(shifted[P - 1:P, 0:C - k],
                             dst[k + (P - 1) * C:E].rearrange("(p c) -> p c", p=1)).then_inc(s_edges, 16)
            sp.dma_start(e_prev[1:P, :], dst[C - 1:E - 1].rearrange("(p c) -> p c", c=C)).then_inc(s_edges, 16)
            sp.dma_start(e_prev[0:1, 1:C], dst[0:C - 1].rearrange("(p c) -> p c", p=1)).then_inc(s_edges, 16)

            def b_load(s):
                if s.plus(-4).exists():
                    sp.wait_ge(b_y, s.plus(-4).times(PAIR, PAIR))
                sp.dma_start(X[:, s.slot(4), :, :], node_rows(x, s)).then_inc(b_ld[s.slot(4)], 16)

            def b_store(s):
                sp.wait_ge(b_out, s.times(PAIR, PAIR))
                if s.at == NG - 1:
                    sp.wait_ge(b_st[s.plus(-1).slot(2)], s.plus(-1).turn(2, 16, 16))
                sp.dma_start(node_rows(out, s), O[:, s.slot(2), :, :]).then_inc(b_st[s.slot(2)], 16)

            def step_b(s):
                if s.plus(3).exists():
                    b_load(s.plus(3))
                if s.plus(-1).exists():
                    b_store(s.plus(-1))

            def step_a(s):
                n = s.plus(4)
                if n.exists():
                    if s.exists():
                        sp.wait_ge(a_prep, s.times(1, 1))
                    for t, rows in enumerate(windows(n)):
                        sp.dma_start(IDX[:, n.slot(4), t, :], rows).then_inc(a_idx[n.slot(4)], 16)

            def fast():
                sp.wait_ge(s_pool0, 2)
                sp.dma_start(dense[MORE:ROWS, :].rearrange("(a r) c -> a (r c)", a=1),
                             tail_rec[0:1, :]).then_inc(s_tail, 16)
                run_steps(sp, NG, 3, step_b)
                b_done(sp)
                sp.wait_ge(s_tail, 16)
                for u in range(UNROLL):
                    sp.wait_ge(b_sc[u], 16 * QUOTA[u] * len(range(u, NG, UNROLL)))
                run_steps(sp, NA, 4, step_a)
                for i in range(2):
                    sp.wait_ge(a_st[i], 16 * PAIR * len(range(i, NA, 2)))

            def general():
                sp.wait_ge(s_setup, 1)
                sp.wait_ge(s_pool0, 2)
                zero = S2[:, :]
                with sp.Fori(0, SROWS // LANES) as i:
                    sp.dma_start(table[bass.ds(i * LANES, LANES), :], zero).then_inc(g_zero, 16)
                sp.wait_ge(g_zero, 16 * (SROWS // LANES))
                with sp.Fori(0, C) as k:
                    sp.wait_ge(g_add, k * 16)
                    sp.dma_start(IDX[0:P, 0, 0, 0:1],
                                 src[bass.ds(k * P, P)].rearrange("(p c) -> p c", c=1)).then_inc(g_ld, 16)
                    sp.dma_start(IDX[0:P, 0, 0, 1:2],
                                 dst[bass.ds(k * P, P)].rearrange("(p c) -> p c", c=1)).then_inc(g_ld, 16)
                sp.wait_ge(g_add, 16 * C)

                def tile(i, base):
                    sp.dma_start(X[:, 0, 0, :], x[base, :]).then_inc(g_in, 16)
                    sp.dma_start(S2[:, :], table[base, :]).then_inc(g_in, 16)
                    sp.wait_ge(g_act, TILE_ACT(i, 5))
                    sp.dma_start(out[base, :], O[:, 0, 0, :]).then_inc(g_st, 16)
                    wait_alone(sp, g_st, i * 16 + 16)

                with sp.Fori(0, NT - 1) as i:
                    tile(i, bass.ds(i * LANES, LANES))
                tile(NT - 1, slice(N - LANES, N))

            when_fast(sp, fast, general)

        @block.gpsimd
        def _(pool):
            pool.memset(ident[:, :], 0.0).then_inc(s_id0, 1)
            pool.memset(ones[:, :], 1.0)
            pool.memset(earlier[:, :], 1.0).then_inc(s_id0, 1)
            pool.wait_ge(s_id0, 2)
            pool.affine_select(out=ident[:, :], in_=ident[:, :], compare_op=ALU.not_equal, fill=1.0,
                               base=0, pattern=[[-1, LANES]], channel_multiplier=1)
            pool.affine_select(out=earlier[:, :], in_=earlier[:, :], compare_op=ALU.is_gt, fill=0.0,
                               base=0, pattern=[[-1, LANES]], channel_multiplier=1)
            pool.iota(e_no[:, :], pattern=[[1, C]], base=0, channel_multiplier=C)
            pool.iota(IDX[:, 0, 0, 0:1], pattern=[[0, 1]], base=0, channel_multiplier=1).then_inc(s_const, 1)
            pool.memset(tail_rec[:, :], FAR)
            pool.memset(STG[:, :, :, :], 0).then_inc(s_pool0, 1)
            pool.memset(S2[:, :], 0.0).then_inc(s_pool0, 1)

            def b_scatter(s):
                q, u = QUOTA[s.slot(UNROLL)], s.slot(UNROLL)
                if not q:
                    return
                col = s.turn(UNROLL, PER_BODY, sum(QUOTA[:u]))
                if s.plus(-UNROLL).exists():
                    pool.wait_ge(b_sc[u], s.turn(UNROLL, 16 * q))
                cols = slice(col, col + q) if s.reg is None else bass.ds(col, q)
                pool.tensor_copy(STG[:, u, 0:q, :], REC[:, cols, :]).then_inc(b_stage, 1)
                wait_alone(pool, b_stage, s.times(1, 1))
                for j in range(q):
                    pool.indirect_dma_start(
                        out=dense[:, :], out_offset=bass.IndirectOffsetOnAxis(ap=STG[:, u, j, 3:4], axis=0),
                        in_=STG[:, u, j, 0:3], in_offset=None,
                        bounds_check=ROWS - 1, oob_is_err=False).then_inc(b_sc[u], 16)

            def step_b(s):
                if s.exists():
                    b_scatter(s)
                n = s.plus(1)
                if n.exists():
                    for t in range(PAIR):
                        pool.wait_ge(b_hi, n.times(PAIR, t + 1))
                        if s.plus(-1).exists():
                            pool.wait_ge(b_z, s.plus(-1).times(PAIR, t + 1))
                        pool.tensor_tensor(XL[:, n.slot(2), t, :], XT[:, n.slot(2), t, :],
                                           XH[:, n.slot(2), t, :].bitcast(f32), ALU.subtract).then_inc(b_lo, 1)

            def gather(to, rows, idx, done):
                pool.indirect_dma_start(out=to, out_offset=None, in_=rows,
                                        in_offset=bass.IndirectOffsetOnAxis(ap=idx, axis=0),
                                        bounds_check=N - 1, oob_is_err=False).then_inc(done, 16)

            def step_a(s):
                n = s.plus(3)
                if n.exists():
                    pool.wait_ge(a_idx[n.slot(4)], n.turn(4, 16 * PAIR, 16 * PAIR))
                    if s.plus(-1).exists():
                        pool.wait_ge(a_y, s.plus(-1).times(PAIR, PAIR))
                    if s.plus(1).exists() and (s.reg is not None or s.at >= -1):
                        wait_alone(pool, a_zg, s.plus(1).times(PAIR, PAIR))
                    for t in range(PAIR):
                        gather(G[:, n.slot(2), t, :], x[:, :], IDX[:, n.slot(4), t, 0:1], a_gg[n.slot(4)])
                        gather(X[:, n.slot(4), t, :], x[:, :], IDX[:, n.slot(4), t, 1:2], a_gx[n.slot(4)])
                n = s.plus(1)
                if n.exists():
                    for t in range(PAIR):
                        pool.wait_ge(a_hi, n.times(PAIR, t + 1))
                        if s.plus(-1).exists():
                            pool.wait_ge(a_z, s.plus(-1).times(PAIR, t + 1))
                        pool.tensor_tensor(XL[:, n.slot(2), t, :], XT[:, n.slot(2), t, :],
                                           XH[:, n.slot(2), t, :].bitcast(f32), ALU.subtract).then_inc(a_lo, 1)
                    for t in range(PAIR):
                        pool.wait_ge(a_sh, n.times(PAIR, t + 1))
                        pool.tensor_tensor(SL[:, n.slot(2), t, :], ST[:, n.slot(2), t, :],
                                           SH[:, n.slot(2), t, :].bitcast(f32), ALU.subtract).then_inc(a_sl, 1)
                n = s.plus(-1)
                if n.exists():
                    for t in range(PAIR):
                        wait_alone(pool, a_out, n.times(PAIR, t + 1))
                        pool.indirect_dma_start(
                            out=out[:, :], out_offset=bass.IndirectOffsetOnAxis(ap=NID[:, n.slot(4), t:t + 1], axis=0),
                            in_=O[:, n.slot(2), t, :], in_offset=None,
                            bounds_check=N - 1, oob_is_err=False).then_inc(a_st[n.slot(2)], 16)

            def fast():
                pool.wait_ge(s_setup, 1)
                run_steps(pool, NG, 3, step_b)
                b_done(pool)
                run_steps(pool, NA, 4, step_a)

            def general():
                pool.wait_ge(s_setup, 1)
                with pool.Fori(0, C) as k:
                    wait_alone(pool, g_ld, k * 32 + 32)
                    gather(G[0:P, 0, 0, :], x[:, :], IDX[0:P, 0, 0, 0:1], g_gat)
                    wait_alone(pool, g_dve, CHUNK_DVE(k, EDGE_DVE))
                    pool.indirect_dma_start(
                        out=table[:, :], out_offset=bass.IndirectOffsetOnAxis(ap=NID[0:P, 0, 0:1], axis=0),
                        in_=S2[0:P, :], in_offset=None, bounds_check=SROWS - 1, oob_is_err=True,
                        compute_op=ALU.add).then_inc(g_add, 16)

            when_fast(pool, fast, general)

        @block.vector
        def _(dve):
            v = nc.vector
            links = [0]

            def link(ins):
                links[0] += 1
                ins.then_inc(s_chain, 1)
                dve.wait_ge(s_chain, links[0])

            v.memset(e_next[:, :], N)
            v.memset(e_prev[:, :], -1)
            v.memset(e_run[:, :], N).then_inc(s_pad, 1)
            v.memset(eps1[:, :], EPS)
            v.memset(eps4[:, :], EPS / 4)
            v.memset(REC[:, :, :], FAR)
            dve.wait_ge(s_edges, 16 * 8)
            dve.wait_ge(s_const, 1)
            link(v.tensor_tensor(f_a[:, :], e_next[:, :], e_d[:, :], ALU.subtract))
            v.tensor_scalar(f_nl[:, :], f_a[:, :], 0.0, None, ALU.is_equal)
            link(v.tensor_scalar(f_b[:, :], f_a[:, :], 1.0, None, ALU.is_equal))
            link(v.tensor_tensor(f_v[:, :], f_nl[:, :], f_b[:, :], ALU.add))
            link(v.tensor_scalar(f_v[:, :], f_v[:, :], -1.0, 1.0, ALU.mult, ALU.add))
            link(v.tensor_tensor(f_a[:, :], e_s[:, :], e_d[:, :], ALU.not_equal))
            link(v.tensor_tensor(f_a[:, :], f_a[:, :], f_b[:, :], ALU.mult))
            link(v.tensor_tensor(f_v[:, :], f_v[:, :], f_a[:, :], ALU.add))
            link(v.tensor_tensor(f_a[:, :], e_run[:, :], e_d[:, :], ALU.is_equal))
            link(v.tensor_tensor(f_v[:, :], f_v[:, :], f_a[:, :], ALU.add))
            link(v.tensor_scalar(f_a[0:1, 0:1], e_d[0:1, 0:1], 0.0, None, ALU.not_equal))
            link(v.tensor_tensor(f_v[0:1, 0:1], f_v[0:1, 0:1], f_a[0:1, 0:1], ALU.add))
            v.reduce_sum(v_sum[:, :], f_v[:, :], AX.X).then_inc(s_viol, 1)
            v.tensor_copy(REC[:, 0:C, 0], e_s[:, :])
            v.tensor_copy(REC[:, 0:C, 1], e_d[:, :])
            link(v.tensor_tensor(f_a[:, :], e_prev[:, :], e_d[:, :], ALU.is_equal))
            link(v.tensor_scalar(f_a[:, :], f_a[:, :], float(FAR), None, ALU.mult))
            link(v.tensor_tensor(REC[:, 0:C, 2], f_a[:, :], e_d[:, :], ALU.add))
            link(v.tensor_scalar(f_nl[:, :], f_nl[:, :], float(-FAR), float(FAR), ALU.mult, ALU.add))
            link(v.tensor_tensor(f_a[:, :], e_no[:, :], e_d[:, :], ALU.subtract))
            link(v.tensor_tensor(REC[:, 0:C, 3], f_a[:, :], f_nl[:, :], ALU.add))
            v.tensor_copy(lane_no[:, :], IDX[:, 0, 0, 0:1]).then_inc(s_viol, 1)
            dve.wait_ge(s_viol, 2)
            for t in range(PAIR):
                link(v.tensor_scalar(slot_far[:, t:t + 1], lane_no[:, :], float(STRIDE), float(FAR),
                                     ALU.is_ge, ALU.mult))
            dve.wait_ge(s_flagp, 1)
            v.tensor_copy(flag[:, :], PT[0][0:1, 0:1]).then_inc(s_flag, 1)
            dve.wait_ge(s_small, 48)
            for k in range(KC):
                v.tensor_copy(bwide[:, k, :], wide(bcol[:, k:k + 1], LANES))
            link(v.tensor_scalar(gcol[:, :], gcol[:, :], 0.5, None, ALU.mult))
            raw = (Y, O)
            scaled = (XT, ZX)
            for w in range(2):
                for k in range(KC):
                    bank = (PS, PL, PR, PT)[k][w]
                    dve.wait_ge(s_wT, w * KC + k + 1)
                    v.tensor_copy(raw[w][:, k // PAIR, k % PAIR, :], bank[:, :])
                    v.tensor_scalar(scaled[w][:, k // PAIR, k % PAIR, :], bank[:, :], gcol[:, k:k + 1], None,
                                    ALU.mult).then_inc(s_wdone, 1)

            def flat(b):
                return b[:, :, :, :].rearrange("p a b d -> p (a b) d")

            dve.wait_ge(s_wdone, 2 * KC)
            link(v.tensor_tensor(flat(G), flat(scaled[0]), flat(scaled[1]), ALU.add))
            for full, hi, lo in ((flat(scaled[0]), wl_hi, wl_lo), (flat(scaled[1]), wr_hi, wr_lo),
                                 (flat(G), ws_hi, ws_lo)):
                link(v.tensor_copy(hi[:, :, :], full))
                v.tensor_tensor(lo[:, :, :], full, hi[:, :, :].bitcast(f32), ALU.subtract)
            dve.wait_ge(s_bias, 1)
            v.tensor_scalar(bias_l[:, :], PS[0][:, :], 0.5, None, ALU.mult)
            link(v.tensor_scalar(bias_r[:, :], PL[0][:, :], 0.5, None, ALU.mult))
            v.memset(SEL[:, :, :, :], 0.0)
            link(v.memset(G[:, :, :, :], 0.0))
            v.tensor_tensor(bias_s[:, :], bias_l[:, :], bias_r[:, :], ALU.add).then_inc(s_setup, 1)

            def norm(mv, sd, rs, nm, slot, sd_ready, rs_done, nm_done, s, per=1, n=0):
                dve.wait_ge(sd_ready, s.times(per, n + 1))
                v.reciprocal(rs[:, slot, :], sd[:, slot, :]).then_inc(rs_done, 1)
                dve.wait_ge(rs_done, s.times(per, n + 1))
                v.scalar_tensor_tensor(out=nm[:, slot, :], in0=mv[:, slot, :, 0], scalar=-1.0,
                                       in1=rs[:, slot, :], op0=ALU.mult, op1=ALU.mult).then_inc(nm_done, 1)

            def y_stats(s, t, y_done, bn_done, var_done):
                dve.wait_ge(y_done, s.times(PAIR, t + 1))
                v.bn_stats(ys[0][:, s.slot(2), t, :], Y[:, s.slot(2), t, :]).then_inc(bn_done, 1)

            def y_aggr(s, t, bn_done, var_done):
                wait_alone(dve, bn_done, s.times(PAIR, t + 1))
                v.bn_aggr(ys[1][:, s.slot(2), t, :], ys[0][:, s.slot(2), t, :]).then_inc(var_done, 1)

            def step_b(s):
                n = s.plus(2)
                if n.exists():
                    dve.wait_ge(b_ld[n.slot(4)], n.turn(4, 16, 16))
                    if s.exists():
                        dve.wait_ge(b_zn, s.times(PAIR, PAIR))
                    for t in range(PAIR):
                        v.bn_stats(xs[0][:, n.slot(2), t, :], X[:, n.slot(4), t, :]).then_inc(b_bn, 1)
                    for t in range(PAIR):
                        wait_alone(dve, b_bn, n.times(PAIR, t + 1))
                        v.bn_aggr(xs[1][:, n.slot(2), t, :], xs[0][:, n.slot(2), t, :]).then_inc(b_var, 1)
                if s.plus(-1).exists():
                    norm(ys[1], ys[2], ys[3], ys[4], s.plus(-1).slot(2), b_ysd, b_yrs, b_ynm, s.plus(-1))
                for t in range(PAIR):
                    if s.exists():
                        y = Y[:, s.slot(2), t, :]
                        dve.wait_ge(b_z, s.times(PAIR, t + 1))
                        if s.plus(-2).exists():
                            dve.wait_ge(b_out, s.plus(-2).times(PAIR, t + 1))
                        v.tensor_tensor(y, PZ[s.slot(2)][t][:, :], bias_s[:, :], ALU.add).then_inc(b_t, 1)
                    if t == 0 and n.exists():
                        norm(xs[1], xs[2], xs[3], xs[4], n.slot(2), b_sd, b_rs, b_nm, n)
                    if s.exists():
                        dve.wait_ge(b_t, s.times(PAIR, t + 1))
                        v.scalar_tensor_tensor(out=y, in0=y, scalar=0.0, in1=X[:, s.slot(4), t, :],
                                               op0=ALU.max, op1=ALU.add).then_inc(b_y, 1)
                if s.exists():
                    for t in range(PAIR):
                        y_stats(s, t, b_y, b_ybn, b_yvar)
                    for t in range(PAIR):
                        y_aggr(s, t, b_ybn, b_yvar)

            def step_a(s):
                n = s.plus(2)
                if n.exists():
                    q = n.slot(4)
                    dve.wait_ge(a_gx[q], n.turn(4, 16 * PAIR, 16 * PAIR))
                    dve.wait_ge(a_gg[q], n.turn(4, 16 * PAIR, 16 * PAIR))
                    if s.exists():
                        dve.wait_ge(a_zg, s.times(PAIR, PAIR))
                    for t in range(PAIR):
                        v.bn_stats(xs[0][:, n.slot(2), t, :], X[:, q, t, :])
                        v.bn_stats(gs[0][:, n.slot(2), t, :], G[:, n.slot(2), t, :]).then_inc(a_bn, 1)
                    for t in range(PAIR):
                        wait_alone(dve, a_bn, n.times(PAIR, t + 1))
                        v.bn_aggr(xs[1][:, n.slot(2), t, :], xs[0][:, n.slot(2), t, :])
                        v.bn_aggr(gs[1][:, n.slot(2), t, :], gs[0][:, n.slot(2), t, :]).then_inc(a_var, 1)
                    if s.exists():
                        dve.wait_ge(a_D, s.times(PAIR, PAIR))
                    if s.plus(-2).exists():
                        dve.wait_ge(a_st[s.slot(2)], s.plus(-2).turn(2, 16 * PAIR, 16 * PAIR))
                    for t in range(PAIR):
                        v.tensor_copy(DB[:, n.slot(2), t, :], wide(IDX[:, q, t, 1:2], LANES))
                    v.tensor_copy(DCF[:, q, :], IDX[:, q, :, 1])
                    v.tensor_tensor(NID[:, q, :], IDX[:, q, :, 2], slot_far[:, :], ALU.add).then_inc(a_prep, 1)
                if s.plus(-1).exists():
                    norm(ys[1], ys[2], ys[3], ys[4], s.plus(-1).slot(2), a_ysd, a_yrs, a_ynm, s.plus(-1))
                m = s.plus(1)
                if m.exists():
                    for t in range(PAIR):
                        dve.wait_ge(a_xt, m.times(PAIR, t + 1))
                        dve.wait_ge(a_S, m.times(PAIR, t + 1))
                        if s.plus(-1).exists():
                            dve.wait_ge(a_sl, s.plus(-1).times(PAIR, t + 1))
                        v.tensor_tensor(ST[:, m.slot(2), t, :], PS[t][:, :], XT[:, m.slot(2), t, :],
                                        ALU.add).then_inc(a_sT, 1)
                for t in range(PAIR):
                    if s.exists():
                        y = Y[:, s.slot(2), t, :]
                        dve.wait_ge(a_z, s.times(PAIR, t + 1))
                        if s.plus(-2).exists():
                            dve.wait_ge(a_out, s.plus(-2).times(PAIR, t + 1))
                        v.scalar_tensor_tensor(out=y, in0=PL[t][:, :], scalar=RC[:, s.slot(4), t:t + 1],
                                               in1=bias_s[:, :], op0=ALU.mult, op1=ALU.add).then_inc(a_t1, 1)
                        dve.wait_ge(a_t1, s.times(PAIR, t + 1))
                        v.tensor_tensor(y, PR[t][:, :], y, ALU.add).then_inc(a_t2, 1)
                        dve.wait_ge(a_t2, s.times(PAIR, t + 1))
                        v.scalar_tensor_tensor(out=y, in0=y, scalar=0.0, in1=X[:, s.slot(4), t, :],
                                               op0=ALU.max, op1=ALU.add).then_inc(a_y, 1)
                    if t == 0 and n.exists():
                        norm(xs[1], xs[2], xs[3], xs[4], n.slot(2), a_sd, a_rs, a_nm, n, 2, 0)
                        norm(gs[1], gs[2], gs[3], gs[4], n.slot(2), a_sd, a_rs, a_nm, n, 2, 1)
                        if s.exists():
                            dve.wait_ge(a_S, s.times(PAIR, PAIR))
                        for r in range(PAIR):
                            dve.wait_ge(a_D, n.times(PAIR, r + 1))
                            v.tensor_scalar(SEL[:, n.slot(2), r, :], PT[r][:, 0:LANES], DCF[:, n.slot(4), r:r + 1],
                                            None, ALU.is_equal).then_inc(a_sel, 1)
                        dve.wait_ge(a_sel, n.times(PAIR, PAIR))
                        v.reduce_sum(CNT[:, n.slot(4), :], SEL[:, n.slot(2), :, :], AX.X).then_inc(a_cnt, 1)
                        dve.wait_ge(a_cnt, n.times(1, 1))
                        v.tensor_scalar(CNT[:, n.slot(4), :], CNT[:, n.slot(4), :], 1.0, None,
                                        ALU.add).then_inc(a_cnt1, 1)
                        dve.wait_ge(a_cnt1, n.times(1, 1))
                        v.reciprocal(RC[:, n.slot(4), :], CNT[:, n.slot(4), :]).then_inc(a_rc, 1)
                if s.exists():
                    for t in range(PAIR):
                        y_stats(s, t, a_y, a_ybn, a_yvar)
                    for t in range(PAIR):
                        y_aggr(s, t, a_ybn, a_yvar)

            def fast():
                run_steps(dve, NG, 3, step_b)
                b_done(dve)
                run_steps(dve, NA, 4, step_a)

            def general():
                def count(at):
                    seen = [0]

                    def then(ins):
                        seen[0] += 1
                        ins.then_inc(g_dve, 1)
                        wait_alone(dve, g_dve, at(seen[0]))
                    return then, seen

                with dve.Fori(0, C) as k:
                    then, seen = count(lambda n: CHUNK_DVE(k, n))
                    dve.wait_ge(g_ld, k * 32 + 32)
                    then(v.tensor_copy(DCF[0:P, 0, 0:1], IDX[0:P, 0, 0, 1:2]))
                    then(v.tensor_copy(DB[0:P, 0, 0, 0:P], wide(IDX[0:P, 0, 0, 1:2], P)))
                    dve.wait_ge(g_gat, k * 16 + 16)
                    then(v.bn_stats(gs[0][0:P, 0, 0, :], G[0:P, 0, 0, :]))
                    then(v.bn_aggr(gs[1][0:P, 0, 0, :], gs[0][0:P, 0, 0, :]))
                    dve.wait_ge(g_act, CHUNK_ACT(k, 1))
                    then(v.reciprocal(gs[3][0:P, 0, 0:1], gs[2][0:P, 0, 0:1]))
                    then(v.scalar_tensor_tensor(out=gs[4][0:P, 0, 0:1], in0=gs[1][0:P, 0, 0, 0:1], scalar=-1.0,
                                                in1=gs[3][0:P, 0, 0:1], op0=ALU.mult, op1=ALU.mult))
                    dve.wait_ge(g_pe, CHUNK_PE(k, 1))
                    then(v.tensor_scalar(SEL[0:P, 0, 0, 0:P], PT[0][0:P, 0:P], DCF[0:P, 0, 0:1], None,
                                         ALU.is_equal))
                    then(v.reduce_sum(S2[0:P, D:D + 1], SEL[0:P, 0, 0, 0:P], AX.X))
                    then(v.tensor_tensor(SEL[0:P, 0, 1, 0:P], SEL[0:P, 0, 0, 0:P], earlier[0:P, 0:P], ALU.mult))
                    then(v.reduce_sum(CNT[0:P, 0, 0:1], SEL[0:P, 0, 1, 0:P], AX.X))
                    then(v.tensor_scalar(CNT[0:P, 0, 0:1], CNT[0:P, 0, 0:1], 0.0, None, ALU.is_gt))
                    then(v.tensor_scalar(RC[0:P, 0, 0:1], lane_no[0:P, :], float(N), None, ALU.add))
                    then(v.tensor_tensor(RC[0:P, 0, 0:1], RC[0:P, 0, 0:1], DCF[0:P, 0, 0:1], ALU.subtract))
                    then(v.tensor_tensor(RC[0:P, 0, 0:1], RC[0:P, 0, 0:1], CNT[0:P, 0, 0:1], ALU.mult))
                    then(v.tensor_tensor(NID[0:P, 0, 0:1], RC[0:P, 0, 0:1], DCF[0:P, 0, 0:1], ALU.add))
                    dve.wait_ge(g_pe, CHUNK_PE(k, 2))
                    then(v.tensor_copy(S2[0:P, 0:D], PL[0][0:P, :]))
                    then(v.memset(SEL[0:P, 0, 1, 0:P], 0.0))
                    assert seen[0] == EDGE_DVE

                def tile(i):
                    then, seen = count(lambda n: TILE_DVE(i, n))
                    dve.wait_ge(g_in, i * 32 + 32)
                    then(v.bn_stats(xs[0][:, 0, 0, :], X[:, 0, 0, :]))
                    then(v.bn_aggr(xs[1][:, 0, 0, :], xs[0][:, 0, 0, :]))
                    then(v.tensor_scalar(CNT[:, 0, 0:1], S2[:, D:D + 1], 1.0, None, ALU.max))
                    then(v.reciprocal(RC[:, 0, 0:1], CNT[:, 0, 0:1]))
                    then(v.tensor_scalar(CNT[:, 0, 1:2], S2[:, D:D + 1], 1.0, None, ALU.min))
                    then(v.tensor_scalar(ZG[:, 0, 0, :], S2[:, 0:D], RC[:, 0, 0:1], None, ALU.mult))
                    dve.wait_ge(g_act, TILE_ACT(i, 1))
                    then(v.reciprocal(xs[3][:, 0, 0:1], xs[2][:, 0, 0:1]))
                    then(v.scalar_tensor_tensor(out=xs[4][:, 0, 0:1], in0=xs[1][:, 0, 0, 0:1], scalar=-1.0,
                                                in1=xs[3][:, 0, 0:1], op0=ALU.mult, op1=ALU.mult))
                    dve.wait_ge(g_act, TILE_ACT(i, 3))
                    v.tensor_tensor(XL[:, 0, 0, :], PT[0][:, :], XH[:, 0, 0, :].bitcast(f32), ALU.subtract)
                    then(v.tensor_tensor(SL[:, 0, 0, :], PS[0][:, :], SH[:, 0, 0, :].bitcast(f32),
                                         ALU.subtract))
                    dve.wait_ge(g_pe, TILE_PE(i, 2))
                    then(v.tensor_tensor(Y[:, 0, 0, :], PL[0][:, :], bias_r[:, :], ALU.add))
                    then(v.scalar_tensor_tensor(out=Y[:, 0, 0, :], in0=bias_l[:, :], scalar=CNT[:, 0, 1:2],
                                                in1=Y[:, 0, 0, :], op0=ALU.mult, op1=ALU.add))
                    then(v.scalar_tensor_tensor(out=Y[:, 0, 0, :], in0=Y[:, 0, 0, :], scalar=0.0,
                                                in1=X[:, 0, 0, :], op0=ALU.max, op1=ALU.add))
                    then(v.bn_stats(ys[0][:, 0, 0, :], Y[:, 0, 0, :]))
                    then(v.bn_aggr(ys[1][:, 0, 0, :], ys[0][:, 0, 0, :]))
                    dve.wait_ge(g_act, TILE_ACT(i, 4))
                    then(v.reciprocal(ys[3][:, 0, 0:1], ys[2][:, 0, 0:1]))
                    then(v.scalar_tensor_tensor(out=ys[4][:, 0, 0:1], in0=ys[1][:, 0, 0, 0:1], scalar=-1.0,
                                                in1=ys[3][:, 0, 0:1], op0=ALU.mult, op1=ALU.mult))
                    assert seen[0] == T_DVE

                with dve.Fori(0, NT - 1) as i:
                    tile(i)
                tile(NT - 1)

            when_fast(dve, fast, general)

        @block.scalar
        def _(act):
            a = nc.scalar

            def sqrt(sd, mv, slot, eps, ready, value, done):
                act.wait_ge(ready, value)
                a.activation(sd[:, slot, :], mv[:, slot, :, 1], ACT.Sqrt, bias=eps[:, 0:1]).then_inc(done, 1)

            def normalized(to, rows, st, slot, t):
                return a.activation(to, rows, ACT.Identity, bias=st[4][:, slot, t:t + 1],
                                    scale=st[3][:, slot, t:t + 1])

            def step_b(s):
                y = s.plus(-1)
                if y.exists():
                    sqrt(ys[2], ys[1], y.slot(2), eps4, b_yvar, y.times(PAIR, PAIR), b_ysd)
                m = s.plus(1)
                if m.exists():
                    for t in range(PAIR):
                        act.wait_ge(b_T, m.times(PAIR, t + 1))
                        if s.plus(-1).exists():
                            act.wait_ge(b_z, s.plus(-1).times(PAIR, t + 1))
                        a.activation(XT[:, m.slot(2), t, :], PT[t][:, :], ACT.Identity).then_inc(b_xt, 1)
                        a.activation(XH[:, m.slot(2), t, :], PT[t][:, :], ACT.Identity).then_inc(b_hi, 1)
                n = s.plus(2)
                if n.exists():
                    sqrt(xs[2], xs[1], n.slot(2), eps1, b_var, n.times(PAIR, PAIR), b_sd)
                if y.exists():
                    act.wait_ge(b_ynm, y.times(1, 1))
                    if s.plus(-3).exists():
                        act.wait_ge(b_st[y.slot(2)], y.turn(2, 16))
                    for t in range(PAIR):
                        normalized(O[:, y.slot(2), t, :], Y[:, y.slot(2), t, :], ys, y.slot(2), t).then_inc(b_out, 1)
                if n.exists():
                    act.wait_ge(b_nm, n.times(1, 1))
                    if s.exists():
                        act.wait_ge(b_T, s.times(PAIR, PAIR))
                    for t in range(PAIR):
                        normalized(ZX[:, n.slot(2), t, :], X[:, n.slot(4), t, :], xs, n.slot(2), t).then_inc(b_zn, 1)

            def step_a(s):
                y = s.plus(-1)
                if y.exists():
                    sqrt(ys[2], ys[1], y.slot(2), eps4, a_yvar, y.times(PAIR, PAIR), a_ysd)
                m = s.plus(1)
                if m.exists():
                    for t in range(PAIR):
                        act.wait_ge(a_T, m.times(PAIR, t + 1))
                        if s.plus(-1).exists():
                            act.wait_ge(a_z, s.plus(-1).times(PAIR, t + 1))
                        a.activation(XT[:, m.slot(2), t, :], PT[t][:, :], ACT.Identity).then_inc(a_xt, 1)
                        a.activation(XH[:, m.slot(2), t, :], PT[t][:, :], ACT.Identity).then_inc(a_hi, 1)
                n = s.plus(2)
                if n.exists():
                    sqrt(xs[2], xs[1], n.slot(2), eps1, a_var, n.times(PAIR, PAIR), a_sd)
                    sqrt(gs[2], gs[1], n.slot(2), eps1, a_var, n.times(PAIR, PAIR), a_sd)
                if m.exists():
                    for t in range(PAIR):
                        act.wait_ge(a_sT, m.times(PAIR, t + 1))
                        a.activation(SH[:, m.slot(2), t, :], ST[:, m.slot(2), t, :], ACT.Identity).then_inc(a_sh, 1)
                if y.exists():
                    act.wait_ge(a_ynm, y.times(1, 1))
                    if s.plus(-3).exists():
                        act.wait_ge(a_st[y.slot(2)], y.turn(2, 16 * PAIR))
                    for t in range(PAIR):
                        normalized(O[:, y.slot(2), t, :], Y[:, y.slot(2), t, :], ys, y.slot(2), t).then_inc(a_out, 1)
                if n.exists():
                    act.wait_ge(a_nm, n.times(2, 2))
                    if s.exists():
                        act.wait_ge(a_S, s.times(PAIR, PAIR))
                    for t in range(PAIR):
                        normalized(ZX[:, n.slot(2), t, :], X[:, n.slot(4), t, :], xs, n.slot(2), t).then_inc(a_zx, 1)
                        normalized(ZG[:, n.slot(2), t, :], G[:, n.slot(2), t, :], gs, n.slot(2), t).then_inc(a_zg, 1)

            def fast():
                run_steps(act, NG, 3, step_b)
                b_done(act)
                run_steps(act, NA, 4, step_a)

            def general():
                with act.Fori(0, C) as k:
                    act.wait_ge(g_dve, CHUNK_DVE(k, 4))
                    a.activation(gs[2][0:P, 0, 0:1], gs[1][0:P, 0, 0, 1:2], ACT.Sqrt,
                                 bias=eps1[0:P, 0:1]).then_inc(g_act, 1)
                    act.wait_ge(g_dve, CHUNK_DVE(k, 6))
                    a.activation(ZG[0:P, 0, 0, :], G[0:P, 0, 0, :], ACT.Identity, bias=gs[4][0:P, 0, 0:1],
                                 scale=gs[3][0:P, 0, 0:1]).then_inc(g_act, 1)

                def tile(i):
                    act.wait_ge(g_dve, TILE_DVE(i, 2))
                    a.activation(xs[2][:, 0, 0:1], xs[1][:, 0, 0, 1:2], ACT.Sqrt, bias=eps1[:, 0:1]).then_inc(g_act, 1)
                    act.wait_ge(g_dve, TILE_DVE(i, 8))
                    normalized(ZX[:, 0, 0, :], X[:, 0, 0, :], xs, 0, 0).then_inc(g_act, 1)
                    act.wait_ge(g_pe, TILE_PE(i, 1))
                    a.activation(XH[:, 0, 0, :], PT[0][:, :], ACT.Identity)
                    a.activation(SH[:, 0, 0, :], PS[0][:, :], ACT.Identity).then_inc(g_act, 1)
                    act.wait_ge(g_dve, TILE_DVE(i, 14))
                    a.activation(ys[2][:, 0, 0:1], ys[1][:, 0, 0, 1:2], ACT.Sqrt, bias=eps4[:, 0:1]).then_inc(g_act, 1)
                    act.wait_ge(g_dve, TILE_DVE(i, 16))
                    normalized(O[:, 0, 0, :], Y[:, 0, 0, :], ys, 0, 0).then_inc(g_act, 1)

                with act.Fori(0, NT - 1) as i:
                    tile(i)
                tile(NT - 1)

            when_fast(act, fast, general)

        @block.tensor
        def _(pe):
            m_ = nc.tensor

            def chunk(b, k):
                return b[:, k * LANES:(k + 1) * LANES]

            def product(bank, hi, lo, w_hi, w_lo, wait_hi, wait_lo, start=True, stop=True):
                wait_hi()
                for k in range(KC):
                    m_.matmul(bank, chunk(hi, k), w_hi[:, k, :], start=start and k == 0, stop=False)
                    m_.matmul(bank, chunk(hi, k), w_lo[:, k, :], start=False, stop=False)
                wait_lo()
                for k in range(KC):
                    last = m_.matmul(bank, chunk(lo, k), w_hi[:, k, :], start=False, stop=stop and k == KC - 1)
                return last

            pe.wait_ge(s_const, 1)
            pe.wait_ge(s_viol, 1)
            m_.matmul(PT[0][0:1, 0:1], v_sum[:, :], ones[0:P, 0:1], start=True, stop=True).then_inc(s_flagp, 1)
            pe.wait_ge(s_w, 32)
            for w, full in enumerate((G, ZG)):
                for k in range(KC):
                    bank = (PS, PL, PR, PT)[k][w]
                    if bank is PT[0]:
                        pe.wait_ge(s_flag, 1)
                    for o in range(KC):
                        last = m_.transpose(chunk(bank, o), chunk(full[:, o // PAIR, o % PAIR, :], k), ident[:, :])
                    last.then_inc(s_wT, 1)
            pe.wait_ge(s_wdone, 2 * KC)
            for k in range(KC):
                m_.matmul(PS[0][:, :], bwide[:, k, :], Y[:, k // PAIR, k % PAIR, :], start=k == 0, stop=k == KC - 1)
            for k in range(KC):
                m_.matmul(PL[0][:, :], bwide[:, k, :], O[:, k // PAIR, k % PAIR, :], start=k == 0, stop=False)
            m_.matmul(PL[0][:, :], ones[0:1, :], blrow[0:1, :], start=False, stop=True).then_inc(s_bias, 1)

            def transposed(bank, rows):
                for k in range(KC):
                    last = m_.transpose(chunk(bank, k), chunk(rows, k), ident[:, :])
                return last

            def step_b(s):
                n = s.plus(1)
                if n.exists():
                    for t in range(PAIR):
                        pe.wait_ge(b_zn, n.times(PAIR, t + 1))
                        if s.exists():
                            pe.wait_ge(b_hi, s.times(PAIR, t + 1))
                        transposed(PT[t], ZX[:, n.slot(2), t, :]).then_inc(b_T, 1)
                if s.exists():
                    for t in range(PAIR):
                        if s.plus(-2).exists():
                            pe.wait_ge(b_t, s.plus(-2).times(PAIR, t + 1))
                        product(PZ[s.slot(2)][t][:, :], XH[:, s.slot(2), t, :], XL[:, s.slot(2), t, :], ws_hi, ws_lo,
                                lambda: pe.wait_ge(b_hi, s.times(PAIR, t + 1)),
                                lambda: pe.wait_ge(b_lo, s.times(PAIR, t + 1))).then_inc(b_z, 1)

            def step_a(s):
                m = s.plus(1)
                if m.exists():
                    for t in range(PAIR):
                        pe.wait_ge(a_zx, m.times(PAIR, t + 1))
                        pe.wait_ge(a_sel, m.times(PAIR, t + 1))
                        transposed(PT[t], ZX[:, m.slot(2), t, :]).then_inc(a_T, 1)
                    for t in range(PAIR):
                        pe.wait_ge(a_zg, m.times(PAIR, t + 1))
                        if s.exists():
                            pe.wait_ge(a_sT, s.times(PAIR, t + 1))
                        for k in range(KC):
                            last = m_.matmul(chunk(PS[t], k), chunk(ZG[:, m.slot(2), t, :], k),
                                             SEL[:, m.slot(2), t, :], start=True, stop=True)
                        last.then_inc(a_S, 1)
                n = s.plus(2)
                for t in range(PAIR):
                    if s.exists():
                        if s.plus(-1).exists():
                            pe.wait_ge(a_t2, s.plus(-1).times(PAIR, t + 1))
                        product(PR[t][:, :], XH[:, s.slot(2), t, :], XL[:, s.slot(2), t, :], wr_hi, wr_lo,
                                lambda: pe.wait_ge(a_hi, s.times(PAIR, t + 1)),
                                lambda: pe.wait_ge(a_lo, s.times(PAIR, t + 1)))
                        product(PL[t][:, :], SH[:, s.slot(2), t, :], SL[:, s.slot(2), t, :], wl_hi, wl_lo,
                                lambda: pe.wait_ge(a_sh, s.times(PAIR, t + 1)),
                                lambda: pe.wait_ge(a_sl, s.times(PAIR, t + 1))).then_inc(a_z, 1)
                    if t == 0 and n.exists():
                        pe.wait_ge(a_prep, n.times(1, 1))
                        for r in range(PAIR):
                            if m.exists():
                                pe.wait_ge(a_hi, m.times(PAIR, r + 1))
                            m_.matmul(PT[r][:, 0:LANES], DB[:, n.slot(2), r, :], ident[:, :],
                                      start=True, stop=True).then_inc(a_D, 1)

            def fast():
                pe.wait_ge(s_setup, 1)
                run_steps(pe, NG, 3, step_b)
                b_done(pe)
                run_steps(pe, NA, 4, step_a)

            def general():
                pe.wait_ge(s_setup, 1)
                with pe.Fori(0, C) as k:
                    pe.wait_ge(g_dve, CHUNK_DVE(k, 2))
                    m_.matmul(PT[0][0:P, 0:P], DB[0:P, 0, 0, 0:P], ident[0:P, 0:P],
                              start=True, stop=True).then_inc(g_pe, 1)
                    pe.wait_ge(g_dve, CHUNK_DVE(k, 7))
                    pe.wait_ge(g_act, CHUNK_ACT(k, 2))
                    m_.matmul(PL[0][0:P, :], SEL[0:P, 0, 0, 0:P], ZG[0:P, 0, 0, :],
                              start=True, stop=True).then_inc(g_pe, 1)

                def tile(i):
                    pe.wait_ge(g_dve, TILE_DVE(i, 8))
                    pe.wait_ge(g_act, TILE_ACT(i, 2))
                    transposed(PT[0], ZX[:, 0, 0, :])
                    transposed(PS[0], ZG[:, 0, 0, :]).then_inc(g_pe, 1)
                    pe.wait_ge(g_dve, TILE_DVE(i, 9))
                    ready = lambda: None
                    product(PL[0][:, :], XH[:, 0, 0, :], XL[:, 0, 0, :], wr_hi, wr_lo, ready, ready, stop=False)
                    product(PL[0][:, :], SH[:, 0, 0, :], SL[:, 0, 0, :], wl_hi, wl_lo, ready, ready,
                            start=False).then_inc(g_pe, 1)

                with pe.Fori(0, NT - 1) as i:
                    tile(i)
                tile(NT - 1)

            when_fast(pe, fast, general)


_INS = ["x", "src", "dst", "L0_gnn_W_l", "L0_gnn_b_l", "L0_gnn_W_r", "L0_gnn_gamma", "L0_gnn_beta"]


def kernel(**inputs):
    import numpy as _np
    import concourse.bacc as _bacc
    from concourse import mybir as _mybir
    from concourse.bass_utils import run_bass_kernel_spmd as _run

    nc = _bacc.Bacc("TRN2", target_bir_lowering=False, num_devices=1)
    arrays, args = {}, []
    for name in _INS:
        a = _np.ascontiguousarray(inputs[name])
        arrays[f"in_{name}"] = a
        args.append(nc.dram_tensor(f"in_{name}", a.shape, _mybir.dt.from_np(a.dtype), kind="ExternalInput").ap())
    shape = arrays["in_x"].shape
    result = nc.dram_tensor("result", shape, _mybir.dt.float32, kind="ExternalOutput").ap()
    gnn_kernel(nc, *args, result)
    r = _run(nc, [arrays], core_ids=[0])
    return r.results[0]["result"]
```

```python
import concourse.bass as bass
from concourse import mybir
from contextlib import ExitStack

LANES = 128
PAIR = 2
UNROLL = 6
WINDOW = 128
STRIDE = 120
RUN = WINDOW - STRIDE + 1
FAR = 1 << 20


class Step:

    def __init__(self, at, total, reg=None):
        self.at, self.total, self.reg = at, total, reg

    def plus(self, k):
        return Step(self.at + k, self.total, self.reg)

    def exists(self):
        return self.reg is not None or 0 <= self.at < self.total

    def times(self, m, k):
        if self.reg is None:
            return m * self.at + k
        return self.reg * (m * UNROLL) + (m * self.at + k)

    def slot(self, n):
        return self.at % n

    def turn(self, n, m=1, k=0):
        if self.reg is None:
            return m * (self.at // n) + k
        return self.reg * (m * (UNROLL // n)) + (m * (self.at // n) + k)


def run_steps(eng, total, ahead, behind, body):
    loops = max(total - 1 - ahead - UNROLL, 0) // UNROLL
    for at in range(-ahead, UNROLL):
        body(Step(at, total))
    if loops:
        with eng.Fori(0, loops) as reg:
            for u in range(UNROLL):
                body(Step(UNROLL + u, total, reg))
    for at in range(UNROLL + UNROLL * loops, total + behind):
        body(Step(at, total))


def gnn_kernel(nc, x, src, dst, w_l, b_l, w_r, gamma, beta, out):
    f32, f32r, i32 = mybir.dt.float32, mybir.dt.float32r, mybir.dt.int32
    ALU, ACT, AX = mybir.AluOpType, mybir.ActivationFunctionType, mybir.AxisListType
    N, D = x.shape
    E = src.shape[0]
    KC = D // LANES
    EPS = 1e-5
    GROUP = PAIR * LANES
    NG = -(-N // GROUP)
    P = max(p for p in range(1, LANES + 1) if E % p == 0)
    C = E // P
    MORE = max(E - N, 0)
    NA = max(-(-MORE // (PAIR * STRIDE)), 1)
    ROWS = NA * PAIR * STRIDE + WINDOW
    BODIES = NG // UNROLL
    PER_BODY = -(-C // BODIES)
    QUOTA = [PER_BODY * (u + 1) // UNROLL - PER_BODY * u // UNROLL for u in range(UNROLL)]
    CPAD = PER_BODY * -(-NG // UNROLL)
    SUMW = D + 4
    NT = -(-N // LANES)
    SROWS = LANES * -(-(N + LANES) // LANES)

    STATW = D + 2
    assert C <= D

    dense = nc.dram_tensor("dense_edges", (ROWS, 3), i32, kind="Internal").ap()
    sums = nc.dram_tensor("pass_b_sums", (N, STATW), f32, kind="Internal").ap()
    table = nc.dram_tensor("sum_table", (SROWS, SUMW), f32, kind="Internal").ap()

    ctx = ExitStack()
    with ctx:
        def sb(name, shape, dt=f32):
            return ctx.enter_context(nc.sbuf_tensor(name, shape, dt))

        def sem(name):
            return ctx.enter_context(nc.semaphore(name))

        wl_hi, wl_lo = sb("wl_hi", [LANES, KC, D], f32r), sb("wl_lo", [LANES, KC, D], f32r)
        wr_hi, wr_lo = sb("wr_hi", [LANES, KC, D], f32r), sb("wr_lo", [LANES, KC, D], f32r)
        ws_hi, ws_lo = sb("ws_hi", [LANES, KC, D], f32r), sb("ws_lo", [LANES, KC, D], f32r)
        bias_l, bias_r, bias_s = sb("bias_l", [LANES, D]), sb("bias_r", [LANES, D]), sb("bias_s", [LANES, D])
        ident, ones = sb("ident", [LANES, LANES]), sb("ones", [LANES, LANES])
        eps1, eps4 = sb("eps1", [LANES, 1]), sb("eps4", [LANES, 1])
        X = sb("x_rows", [LANES, UNROLL, PAIR, D])
        G = sb("src_rows", [LANES, 2, PAIR, D])
        ZX = sb("z_rows", [LANES, 2, PAIR, D])
        ZG = sb("z_src", [LANES, 2, PAIR, D])
        XT = sb("z_T", [LANES, 2, PAIR, D])
        T = sb("sums", [LANES, UNROLL, PAIR, STATW])
        XH, XL = sb("z_T_hi", [LANES, 2, PAIR, D], f32r), sb("z_T_lo", [LANES, 2, PAIR, D], f32r)
        SH, SL = sb("mean_T_hi", [LANES, D], f32r), sb("mean_T_lo", [LANES, D], f32r)
        Y = sb("y_rows", [LANES, 2, PAIR, D])
        O = sb("out_rows", [LANES, 2, PAIR, D])
        SEL = sb("same_dst", [LANES, 2, PAIR, LANES])
        DB = sb("dst_wide", [LANES, 2, PAIR, LANES])

        def stats(name, slots=2):
            both = sb(name + "_rs_nm", [LANES, slots, PAIR, 2])
            return (sb(name + "_bn", [LANES, 2, PAIR, 6]), sb(name + "_mv", [LANES, 2, PAIR, 2]),
                    sb(name + "_sd", [LANES, 2, PAIR]), both[:, :, :, 0], both[:, :, :, 1], both, slots)

        xs, gs, ys = stats("xst", UNROLL), stats("gst"), stats("yst")
        IDX = sb("edge_idx", [LANES, UNROLL, PAIR, 3], i32)
        NID = sb("node_idx", [LANES, UNROLL, PAIR], i32)
        DCF = sb("dst_f", [LANES, UNROLL, PAIR])
        CNT, RC = sb("count", [LANES, 2, PAIR]), sb("rcount", [LANES, 2, PAIR])
        slot_far = sb("slot_far", [LANES, PAIR])
        lane_no = sb("lane_no", [LANES, 1])
        earlier = sb("earlier", [LANES, LANES])
        def copy_of_list(i):
            return T[0:P, 2 + i // PAIR, i % PAIR, 0:C]

        e_d, e_s, e_next = (copy_of_list(i).bitcast(i32) for i in range(3))
        e_prev, e_run, e_no = (sb(name, [P, C], i32) for name in ("e_prev", "e_run", "e_no"))
        f_a, f_b, f_v, f_nl = (copy_of_list(i) for i in range(4, 8))
        v_sum = sb("v_sum", [P, 1])
        flag = sb("flag", [1, 1], i32)
        REC = sb("records", [P, CPAD, 4], i32)
        STG = sb("rec_stage", [P, UNROLL, max(QUOTA), 4], i32)
        tail_rec = sb("tail_rec", [1, (ROWS - MORE) * 3], i32)
        gcol, bcol = sb("gamma_col", [LANES, KC]), sb("beta_col", [LANES, KC])
        blrow = sb("bl_row", [1, D])
        S2 = sb("sum_rows", [LANES, SUMW])
        bwide = T[:, 1, 0, 0:D].rearrange("p (k c) -> p k c", c=LANES)

        PT = [ctx.enter_context(nc.psum_tensor(f"pT{t}", [LANES, D], f32)) for t in range(PAIR)]
        PS = [ctx.enter_context(nc.psum_tensor(f"pS{t}", [LANES, D], f32)) for t in range(PAIR)]
        PL = [ctx.enter_context(nc.psum_tensor(f"pL{t}", [LANES, D], f32)) for t in range(PAIR)]
        PR = [ctx.enter_context(nc.psum_tensor(f"pR{t}", [LANES, D], f32)) for t in range(PAIR)]
        PZ = [PL, PR]

        s_w, s_edges, s_small = sem("weights_in"), sem("edges_in"), sem("small_in")
        s_pad, s_id0, s_const = sem("edge_pads_set"), sem("ident_zeroed"), sem("constants_set")
        s_wT, s_wdone, s_bias, s_setup = sem("weights_T"), sem("weights_split"), sem("bias_psum"), sem("setup_done")
        s_chain, s_viol, s_flagp, s_flag = sem("dve_setup_chain"), sem("violations"), sem("flag_psum"), sem("flag_set")
        s_passed = sem("waits_passed")
        s_tail, s_pool0 = sem("tail_written"), sem("pool_setup_chain")
        b_ld = [sem(f"b_x_in{i}") for i in range(UNROLL)]
        b_st = [sem(f"b_out_stored{i}") for i in range(2)]
        b_ts = [sem(f"b_sums_stored{i}") for i in range(2)]
        b_bn, b_var, b_sd, b_rs, b_nm = (sem("b_x_" + n) for n in ("bn", "var", "sd", "rs", "nm"))
        b_zn, b_T, b_xt, b_hi, b_lo, b_z = (sem("b_" + n) for n in ("z_rows", "z_T_psum", "z_T", "hi", "lo", "product"))
        b_t, b_y, b_ybn, b_yvar, b_ysd, b_yrs, b_ynm, b_out = (
            sem("b_" + n) for n in ("biased", "y", "y_bn", "y_var", "y_sd", "y_rs", "y_nm", "out"))
        b_stage = sem("b_records_staged")
        b_sc = [sem(f"b_scattered{i}") for i in range(UNROLL)]
        a_idx = [sem(f"a_idx_in{i}") for i in range(UNROLL)]
        a_gx = [sem(f"a_x_gathered{i}") for i in range(UNROLL)]
        a_gg = [sem(f"a_src_gathered{i}") for i in range(UNROLL)]
        a_gt = [sem(f"a_sums_gathered{i}") for i in range(UNROLL)]
        a_st = [sem(f"a_out_scattered{i}") for i in range(2)]
        a_bn, a_var, a_sd, a_rs, a_nm = (sem("a_in_" + n) for n in ("bn", "var", "sd", "rs", "nm"))
        a_prep, a_D, a_sel, a_cnt, a_cnt1, a_rc = (
            sem("a_" + n) for n in ("dst_ready", "dst_psum", "same_dst", "count_psum", "count", "rcount"))
        a_zx, a_zg, a_U, a_hi, a_lo, a_z = (
            sem("a_" + n) for n in ("z_rows", "z_src", "diff_sum_T", "hi", "lo", "product"))
        a_t1, a_y, a_ybn, a_yvar, a_ysd, a_yrs, a_ynm, a_out = (
            sem("a_" + n) for n in ("total", "y", "y_bn", "y_var", "y_sd", "y_rs", "y_nm", "out"))
        g_zero, g_ld, g_gat, g_add = sem("g_zeroed"), sem("g_edges_in"), sem("g_gathered"), sem("g_added")
        g_dve, g_act, g_pe = sem("g_dve"), sem("g_act"), sem("g_pe")
        g_in, g_st = sem("g_rows_in"), sem("g_stored")

        block = ctx.enter_context(nc.Block())

        def wide(ap, n):
            return ap.to_broadcast([ap.shape[0], n])

        def node_rows(dram, s):
            if s.reg is None:
                base = min(s.at * GROUP, N - GROUP)
                rows = dram[base:base + GROUP, :]
            else:
                rows = dram[bass.ds(s.times(GROUP, 0), GROUP), :]
            return rows.rearrange("(p t) d -> p t d", t=PAIR)

        def windows(s):
            def one(t):
                if s.reg is None:
                    b = s.at * PAIR * STRIDE + t * STRIDE
                    return dense[b:b + WINDOW, :]
                return dense[bass.ds(s.times(PAIR * STRIDE, t * STRIDE), WINDOW), :]
            return [one(t) for t in range(PAIR)]

        def b_done(eng):
            for i in range(2):
                eng.wait_ge(b_st[i], 16 * len(range(i, NG, 2)))
                eng.wait_ge(b_ts[i], 16 * len(range(i, NG, 2)))

        def scatters(i):
            return PER_BODY * (i // UNROLL) + sum(QUOTA[:i % UNROLL]) < C

        def wait_alone(eng, semaphore, value):
            eng.wait_ge(semaphore, value)
            eng.sem_inc(s_passed, 1)

        def when_fast(eng, fast, general):
            eng.wait_ge(s_flag, 1)
            bad = eng.value_load(flag[0:1, 0:1], min_val=0, max_val=4 * E)
            with eng.If(bad == 0):
                fast()
            with eng.Else():
                general()

        EDGE_DVE, EDGE_ACT, EDGE_PE = 17, 2, 2
        T_DVE, T_ACT, T_PE = 16, 5, 2

        def CHUNK_DVE(k, n):
            return k * EDGE_DVE + n

        def CHUNK_ACT(k, n):
            return k * EDGE_ACT + n

        def CHUNK_PE(k, n):
            return k * EDGE_PE + n

        def TILE_DVE(i, n):
            return i * T_DVE + (C * EDGE_DVE + n)

        def TILE_ACT(i, n):
            return i * T_ACT + (C * EDGE_ACT + n)

        def TILE_PE(i, n):
            return i * T_PE + (C * EDGE_PE + n)

        @block.sync
        def _(sp):
            sp.dma_start(G[:, :, :, :].rearrange("p a b d -> p (a b) d"),
                         w_l.rearrange("(k p) i -> p k i", p=LANES)).then_inc(s_w, 16)
            sp.dma_start(ZG[:, :, :, :].rearrange("p a b d -> p (a b) d"),
                         w_r.rearrange("(k p) i -> p k i", p=LANES)).then_inc(s_w, 16)
            sp.dma_start(gcol[:, :], gamma.rearrange("(k p) -> p k", p=LANES),
                         allow_slow_non_contiguous=True).then_inc(s_small, 16)
            sp.dma_start(bcol[:, :], beta.rearrange("(k p) -> p k", p=LANES),
                         allow_slow_non_contiguous=True).then_inc(s_small, 16)
            sp.dma_start(blrow[0:1, :], b_l.rearrange("(a d) -> a d", a=1)).then_inc(s_small, 16)
            sp.dma_start(e_d[:, :], dst.rearrange("(p c) -> p c", c=C)).then_inc(s_edges, 16)
            sp.dma_start(e_s[:, :], src.rearrange("(p c) -> p c", c=C)).then_inc(s_edges, 16)
            sp.wait_ge(s_pad, 1)
            for shifted, k in ((e_next, 1), (e_run, RUN + 1)):
                sp.dma_start(shifted[0:P - 1, :],
                             dst[k:k + (P - 1) * C].rearrange("(p c) -> p c", c=C)).then_inc(s_edges, 16)
                sp.dma_start(shifted[P - 1:P, 0:C - k],
                             dst[k + (P - 1) * C:E].rearrange("(p c) -> p c", p=1)).then_inc(s_edges, 16)
            sp.dma_start(e_prev[1:P, :], dst[C - 1:E - 1].rearrange("(p c) -> p c", c=C)).then_inc(s_edges, 16)
            sp.dma_start(e_prev[0:1, 1:C], dst[0:C - 1].rearrange("(p c) -> p c", p=1)).then_inc(s_edges, 16)

            def b_load(s):
                if s.plus(-UNROLL).exists():
                    sp.wait_ge(b_y, s.plus(-UNROLL).times(PAIR, PAIR))
                sp.dma_start(X[:, s.slot(UNROLL), :, :], node_rows(x, s)).then_inc(b_ld[s.slot(UNROLL)], 16)

            def b_store_sums(s):
                sp.wait_ge(b_t, s.times(PAIR, PAIR))
                if s.at == NG - 1:
                    sp.wait_ge(b_ts[s.plus(-1).slot(2)], s.plus(-1).turn(2, 16, 16))
                sp.dma_start(node_rows(sums, s), T[:, s.slot(2), :, :]).then_inc(b_ts[s.slot(2)], 16)

            def b_store(s):
                sp.wait_ge(b_out, s.times(PAIR, PAIR))
                if s.at == NG - 1:
                    sp.wait_ge(b_st[s.plus(-1).slot(2)], s.plus(-1).turn(2, 16, 16))
                sp.dma_start(node_rows(out, s), O[:, s.slot(2), :, :]).then_inc(b_st[s.slot(2)], 16)

            def a_load(n):
                old = n.plus(-UNROLL)
                if old.exists():
                    for done in (a_gx, a_gg, a_gt):
                        wait_alone(sp, done[n.slot(UNROLL)], n.turn(UNROLL, 16 * PAIR))
                    wait_alone(sp, a_prep, old.times(1, 1))
                for t, rows in enumerate(windows(n)):
                    sp.dma_start(IDX[:, n.slot(UNROLL), t, :], rows).then_inc(a_idx[n.slot(UNROLL)], 16)

            def step_b(s):
                if s.plus(5).exists():
                    b_load(s.plus(5))
                if s.plus(-2).exists():
                    b_store(s.plus(-2))
                if s.exists():
                    b_store_sums(s)
                if s.at == NG - 2 and s.reg is None:
                    sp.wait_ge(s_tail, 16)
                    for u in range(UNROLL):
                        sp.wait_ge(b_sc[u], 16 * QUOTA[u] * len([i for i in range(u, NG, UNROLL) if scatters(i)]))
                    for n in range(min(5, NA)):
                        a_load(Step(n, NA))

            def step_a(s):
                n = s.plus(5)
                if n.exists() and (s.reg is not None or s.at >= 0):
                    a_load(n)

            def fast():
                sp.wait_ge(s_pool0, 2)
                sp.dma_start(dense[MORE:ROWS, :].rearrange("(a r) c -> a (r c)", a=1),
                             tail_rec[0:1, :]).then_inc(s_tail, 16)
                run_steps(sp, NG, 5, 2, step_b)
                run_steps(sp, NA, 5, 2, step_a)
                for i in range(2):
                    sp.wait_ge(a_st[i], 16 * PAIR * len(range(i, NA, 2)))

            def general():
                sp.wait_ge(s_setup, 1)
                sp.wait_ge(s_pool0, 2)
                zero = S2[:, :]
                with sp.Fori(0, SROWS // LANES) as i:
                    sp.dma_start(table[bass.ds(i * LANES, LANES), :], zero).then_inc(g_zero, 16)
                sp.wait_ge(g_zero, 16 * (SROWS // LANES))
                with sp.Fori(0, C) as k:
                    sp.dma_start(IDX[0:P, 0, 0, 0:1],
                                 src[bass.ds(k * P, P)].rearrange("(p c) -> p c", c=1)).then_inc(g_ld, 16)
                    sp.dma_start(IDX[0:P, 0, 0, 1:2],
                                 dst[bass.ds(k * P, P)].rearrange("(p c) -> p c", c=1)).then_inc(g_ld, 16)
                    wait_alone(sp, g_add, k * 16 + 16)

                def tile(i, base):
                    sp.dma_start(X[:, 0, 0, :], x[base, :]).then_inc(g_in, 16)
                    sp.dma_start(S2[:, :], table[base, :]).then_inc(g_in, 16)
                    sp.wait_ge(g_act, TILE_ACT(i, 5))
                    sp.dma_start(out[base, :], O[:, 0, 0, :]).then_inc(g_st, 16)
                    wait_alone(sp, g_st, i * 16 + 16)

                with sp.Fori(0, NT - 1) as i:
                    tile(i, bass.ds(i * LANES, LANES))
                tile(NT - 1, slice(N - LANES, N))

            when_fast(sp, fast, general)

        @block.gpsimd
        def _(pool):
            pool.memset(ident[:, :], 0.0).then_inc(s_id0, 1)
            pool.memset(ones[:, :], 1.0)
            pool.memset(earlier[:, :], 1.0).then_inc(s_id0, 1)
            pool.wait_ge(s_id0, 2)
            pool.affine_select(out=ident[:, :], in_=ident[:, :], compare_op=ALU.not_equal, fill=1.0,
                               base=0, pattern=[[-1, LANES]], channel_multiplier=1)
            pool.affine_select(out=earlier[:, :], in_=earlier[:, :], compare_op=ALU.is_gt, fill=0.0,
                               base=0, pattern=[[-1, LANES]], channel_multiplier=1)
            pool.iota(e_no[:, :], pattern=[[1, C]], base=0, channel_multiplier=C)
            pool.iota(IDX[:, 0, 0, 0:1], pattern=[[0, 1]], base=0, channel_multiplier=1).then_inc(s_const, 1)
            pool.memset(tail_rec[:, :], FAR)
            pool.memset(STG[:, :, :, :], 0).then_inc(s_pool0, 1)
            pool.memset(S2[:, :], 0.0).then_inc(s_pool0, 1)
            pool.wait_ge(s_viol, 2)
            pool.memset(T[:, 2:, :, :], 0.0).then_inc(s_pool0, 1)

            def b_scatter(s):
                q, u = QUOTA[s.slot(UNROLL)], s.slot(UNROLL)
                if not q or s.reg is None and not scatters(s.at):
                    return
                col = s.turn(UNROLL, PER_BODY, sum(QUOTA[:u]))
                if s.plus(-UNROLL).exists():
                    pool.wait_ge(b_sc[u], s.turn(UNROLL, 16 * q))
                cols = slice(col, col + q) if s.reg is None else bass.ds(col, q)
                pool.tensor_copy(STG[:, u, 0:q, :], REC[:, cols, :]).then_inc(b_stage, 1)
                wait_alone(pool, b_stage, s.times(1, 1))
                for j in range(q):
                    pool.indirect_dma_start(
                        out=dense[:, :], out_offset=bass.IndirectOffsetOnAxis(ap=STG[:, u, j, 3:4], axis=0),
                        in_=STG[:, u, j, 0:3], in_offset=None,
                        bounds_check=ROWS - 1, oob_is_err=False).then_inc(b_sc[u], 16)

            def step_b(s):
                if s.exists():
                    b_scatter(s)
                n = s.plus(1)
                if n.exists():
                    for t in range(PAIR):
                        pool.wait_ge(b_hi, n.times(PAIR, t + 1))
                        if s.plus(-1).exists():
                            pool.wait_ge(b_z, s.plus(-1).times(PAIR, t + 1))
                        pool.tensor_tensor(XL[:, n.slot(2), t, :], XT[:, n.slot(2), t, :],
                                           XH[:, n.slot(2), t, :].bitcast(f32), ALU.subtract).then_inc(b_lo, 1)

            def gather(to, rows, idx, done):
                pool.indirect_dma_start(out=to, out_offset=None, in_=rows,
                                        in_offset=bass.IndirectOffsetOnAxis(ap=idx, axis=0),
                                        bounds_check=N - 1, oob_is_err=False).then_inc(done, 16)

            def gather_rows(n):
                q = n.slot(UNROLL)
                pool.wait_ge(a_idx[q], n.turn(UNROLL, 16 * PAIR, 16 * PAIR))
                if n.plus(-UNROLL).exists():
                    wait_alone(pool, a_y, n.plus(-UNROLL).times(PAIR, PAIR))
                for t in range(PAIR):
                    gather(X[:, q, t, :], x[:, :], IDX[:, q, t, 1:2], a_gx[q])

            def gather_sources(n):
                q = n.slot(UNROLL)
                if n.plus(-2).exists():
                    wait_alone(pool, a_zg, n.plus(-2).times(PAIR, PAIR))
                for t in range(PAIR):
                    gather(G[:, n.slot(2), t, :], x[:, :], IDX[:, q, t, 0:1], a_gg[q])

            def gather_sums(n):
                q = n.slot(UNROLL)
                if n.plus(-UNROLL).exists():
                    wait_alone(pool, a_t1, n.plus(-UNROLL).times(PAIR, PAIR))
                for t in range(PAIR):
                    gather(T[:, q, t, :], sums[:, :], IDX[:, q, t, 1:2], a_gt[q])

            EARLY = min(2, NA)

            def step_a(s):
                n, y = s.plus(4), s.plus(-2)
                if n.exists() and (s.reg is not None or n.at >= EARLY):
                    gather_rows(n)
                    gather_sums(n)
                if y.exists():
                    for t in range(PAIR):
                        wait_alone(pool, a_out, y.times(PAIR, t + 1))
                        pool.indirect_dma_start(
                            out=out[:, :], out_offset=bass.IndirectOffsetOnAxis(ap=NID[:, y.slot(UNROLL), t:t + 1], axis=0),
                            in_=O[:, y.slot(2), t, :], in_offset=None,
                            bounds_check=N - 1, oob_is_err=False).then_inc(a_st[y.slot(2)], 16)
                if n.exists() and (s.reg is not None or n.at >= EARLY):
                    gather_sources(n)

            def fast():
                pool.wait_ge(s_setup, 1)
                run_steps(pool, NG, 5, 2, step_b)
                for n in range(EARLY):
                    wait_alone(pool, a_idx[n], 16 * PAIR)
                    gather_sources(Step(n, NA))
                wait_alone(pool, b_y, NG * PAIR)
                for n in range(EARLY):
                    gather_rows(Step(n, NA))
                b_done(pool)
                for n in range(EARLY):
                    gather_sums(Step(n, NA))
                run_steps(pool, NA, 5, 2, step_a)

            def general():
                pool.wait_ge(s_setup, 1)
                with pool.Fori(0, C) as k:
                    wait_alone(pool, g_ld, k * 32 + 32)
                    gather(G[0:P, 0, 0, :], x[:, :], IDX[0:P, 0, 0, 0:1], g_gat)
                    wait_alone(pool, g_dve, CHUNK_DVE(k, EDGE_DVE))
                    pool.indirect_dma_start(
                        out=table[:, :], out_offset=bass.IndirectOffsetOnAxis(ap=NID[0:P, 0, 0:1], axis=0),
                        in_=S2[0:P, :], in_offset=None, bounds_check=SROWS - 1, oob_is_err=True,
                        compute_op=ALU.add).then_inc(g_add, 16)

            when_fast(pool, fast, general)

        @block.vector
        def _(dve):
            v = nc.vector
            links = [0]

            def link(ins):
                links[0] += 1
                ins.then_inc(s_chain, 1)
                dve.wait_ge(s_chain, links[0])

            v.memset(e_next[:, :], N)
            v.memset(e_prev[:, :], -1)
            v.memset(e_run[:, :], N).then_inc(s_pad, 1)
            v.memset(eps1[:, :], EPS)
            v.memset(eps4[:, :], EPS / 4)
            v.memset(REC[:, :, :], FAR)
            dve.wait_ge(s_edges, 16 * 8)
            dve.wait_ge(s_const, 1)
            link(v.tensor_tensor(f_a[:, :], e_next[:, :], e_d[:, :], ALU.subtract))
            v.tensor_scalar(f_nl[:, :], f_a[:, :], 0.0, None, ALU.is_equal)
            link(v.tensor_scalar(f_b[:, :], f_a[:, :], 1.0, None, ALU.is_equal))
            link(v.tensor_tensor(f_v[:, :], f_nl[:, :], f_b[:, :], ALU.add))
            link(v.tensor_scalar(f_v[:, :], f_v[:, :], -1.0, 1.0, ALU.mult, ALU.add))
            link(v.tensor_tensor(f_a[:, :], e_s[:, :], e_d[:, :], ALU.not_equal))
            link(v.tensor_tensor(f_a[:, :], f_a[:, :], f_b[:, :], ALU.mult))
            link(v.tensor_tensor(f_v[:, :], f_v[:, :], f_a[:, :], ALU.add))
            link(v.tensor_tensor(f_a[:, :], e_run[:, :], e_d[:, :], ALU.is_equal))
            link(v.tensor_tensor(f_v[:, :], f_v[:, :], f_a[:, :], ALU.add))
            link(v.tensor_scalar(f_a[0:1, 0:1], e_d[0:1, 0:1], 0.0, None, ALU.not_equal))
            link(v.tensor_tensor(f_v[0:1, 0:1], f_v[0:1, 0:1], f_a[0:1, 0:1], ALU.add))
            v.reduce_sum(v_sum[:, :], f_v[:, :], AX.X).then_inc(s_viol, 1)
            v.tensor_copy(REC[:, 0:C, 0], e_s[:, :])
            v.tensor_copy(REC[:, 0:C, 1], e_d[:, :])
            link(v.tensor_tensor(f_a[:, :], e_prev[:, :], e_d[:, :], ALU.is_equal))
            link(v.tensor_scalar(f_a[:, :], f_a[:, :], float(FAR), None, ALU.mult))
            link(v.tensor_tensor(REC[:, 0:C, 2], f_a[:, :], e_d[:, :], ALU.add))
            link(v.tensor_scalar(f_nl[:, :], f_nl[:, :], float(-FAR), float(FAR), ALU.mult, ALU.add))
            link(v.tensor_tensor(f_a[:, :], e_no[:, :], e_d[:, :], ALU.subtract))
            link(v.tensor_tensor(REC[:, 0:C, 3], f_a[:, :], f_nl[:, :], ALU.add))
            v.tensor_copy(lane_no[:, :], IDX[:, 0, 0, 0:1]).then_inc(s_viol, 1)
            dve.wait_ge(s_viol, 2)
            for t in range(PAIR):
                link(v.tensor_scalar(slot_far[:, t:t + 1], lane_no[:, :], float(STRIDE), float(FAR),
                                     ALU.is_ge, ALU.mult))
            dve.wait_ge(s_flagp, 1)
            v.tensor_copy(flag[:, :], PT[0][0:1, 0:1]).then_inc(s_flag, 1)
            dve.wait_ge(s_small, 48)
            for k in range(KC):
                v.tensor_copy(bwide[:, k, :], wide(bcol[:, k:k + 1], LANES))
            link(v.tensor_scalar(gcol[:, :], gcol[:, :], 0.5, None, ALU.mult))
            raw = (Y, O)
            scaled = (XT, ZX)
            for w in range(2):
                for k in range(KC):
                    bank = (PS, PL, PR, PT)[k][w]
                    dve.wait_ge(s_wT, w * KC + k + 1)
                    v.tensor_copy(raw[w][:, k // PAIR, k % PAIR, :], bank[:, :])
                    v.tensor_scalar(scaled[w][:, k // PAIR, k % PAIR, :], bank[:, :], gcol[:, k:k + 1], None,
                                    ALU.mult).then_inc(s_wdone, 1)

            def flat(b):
                return b[:, :, :, :].rearrange("p a b d -> p (a b) d")

            dve.wait_ge(s_wdone, 2 * KC)
            link(v.tensor_tensor(flat(G), flat(scaled[0]), flat(scaled[1]), ALU.add))
            for full, hi, lo in ((flat(scaled[0]), wl_hi, wl_lo), (flat(scaled[1]), wr_hi, wr_lo),
                                 (flat(G), ws_hi, ws_lo)):
                link(v.tensor_copy(hi[:, :, :], full))
                v.tensor_tensor(lo[:, :, :], full, hi[:, :, :].bitcast(f32), ALU.subtract)
            dve.wait_ge(s_bias, 1)
            v.tensor_scalar(bias_l[:, :], PS[0][:, :], 0.5, None, ALU.mult)
            link(v.tensor_scalar(bias_r[:, :], PL[0][:, :], 0.5, None, ALU.mult))
            v.memset(SEL[:, :, :, :], 0.0)
            link(v.memset(G[:, :, :, :], 0.0))
            v.tensor_tensor(bias_s[:, :], bias_l[:, :], bias_r[:, :], ALU.add).then_inc(s_setup, 1)

            def reciprocal(st, s, sd_ready, done):
                wait_alone(dve, sd_ready, s.times(1, 1))
                return v.reciprocal(st[3][:, s.slot(st[6]), :], st[2][:, s.slot(2), :]).then_inc(done, 1)

            def minus_mean(st, s, rs_done, done):
                dve.wait_ge(rs_done, s.times(1, 1))
                v.scalar_tensor_tensor(out=st[4][:, s.slot(st[6]), :], in0=st[1][:, s.slot(2), :, 0], scalar=-1.0,
                                       in1=st[3][:, s.slot(st[6]), :], op0=ALU.mult, op1=ALU.mult).then_inc(done, 1)

            def y_stats(s, t, y_done, bn_done):
                dve.wait_ge(y_done, s.times(PAIR, t + 1))
                v.bn_stats(ys[0][:, s.slot(2), t, :], Y[:, s.slot(2), t, :]).then_inc(bn_done, 1)

            def y_aggr(s, t, bn_done, var_done):
                wait_alone(dve, bn_done, s.times(PAIR, t + 1))
                v.bn_aggr(ys[1][:, s.slot(2), t, :], ys[0][:, s.slot(2), t, :]).then_inc(var_done, 1)

            def step_b(s):
                n, e = s.plus(3), s.plus(-1)
                slot = s.slot(2)

                def total(t):
                    dve.wait_ge(b_z, s.times(PAIR, t + 1))
                    if s.plus(-2).exists() and t == 0:
                        dve.wait_ge(b_ts[slot], s.turn(2, 16))
                    v.tensor_tensor(T[:, slot, t, 0:D], PZ[slot][t][:, :], bias_s[:, :], ALU.add).then_inc(b_t, 1)

                def rectified(t):
                    if s.plus(-2).exists():
                        dve.wait_ge(b_out, s.plus(-2).times(PAIR, t + 1))
                    dve.wait_ge(b_t, s.times(PAIR, t + 1))
                    v.scalar_tensor_tensor(out=Y[:, slot, t, :], in0=T[:, slot, t, 0:D], scalar=0.0,
                                           in1=X[:, s.slot(UNROLL), t, :], op0=ALU.max, op1=ALU.add).then_inc(b_y, 1)

                def x_stats(t):
                    if t == 0:
                        dve.wait_ge(b_ld[n.slot(UNROLL)], n.turn(UNROLL, 16, 16))
                        if s.plus(1).exists():
                            dve.wait_ge(b_zn, s.plus(1).times(PAIR, PAIR))
                    v.bn_stats(xs[0][:, n.slot(2), t, :], X[:, n.slot(UNROLL), t, :]).then_inc(b_bn, 1)

                if s.exists():
                    total(0)
                if e.exists():
                    reciprocal(ys, e, b_ysd, b_yrs)
                if s.exists():
                    v.tensor_scalar(T[:, slot, :, D:STATW], xs[5][:, s.slot(UNROLL), :, :], -1.0, None,
                                    ALU.mult)
                    rectified(0)
                if e.exists():
                    minus_mean(ys, e, b_yrs, b_ynm)
                if s.exists():
                    total(1)
                if n.exists():
                    x_stats(0)
                if s.exists():
                    rectified(1)
                if n.exists():
                    x_stats(1)
                if s.exists():
                    y_stats(s, 0, b_y, b_ybn)
                if n.exists():
                    for t in range(PAIR):
                        wait_alone(dve, b_bn, n.times(PAIR, t + 1))
                        v.bn_aggr(xs[1][:, n.slot(2), t, :], xs[0][:, n.slot(2), t, :]).then_inc(b_var, 1)
                if s.exists():
                    y_stats(s, 1, b_y, b_ybn)
                if n.exists():
                    reciprocal(xs, n, b_sd, b_rs)
                if s.exists():
                    y_aggr(s, 0, b_ybn, b_yvar)
                if n.exists():
                    minus_mean(xs, n, b_rs, b_nm)
                if s.exists():
                    y_aggr(s, 1, b_ybn, b_yvar)

            def step_a(s):
                e, m, n, g = s.plus(-1), s.plus(1), s.plus(2), s.plus(3)
                slot, q = s.slot(2), s.slot(UNROLL)

                def total(t):
                    if t == 0:
                        dve.wait_ge(a_gt[q], s.turn(UNROLL, 16 * PAIR, 16 * PAIR))
                        dve.wait_ge(a_rc, s.times(1, 1))
                    dve.wait_ge(a_z, s.times(PAIR, t + 1))
                    if s.plus(-2).exists():
                        dve.wait_ge(a_out, s.plus(-2).times(PAIR, t + 1))
                    v.scalar_tensor_tensor(out=Y[:, slot, t, :], in0=PZ[slot][t][:, :], scalar=RC[:, slot, t:t + 1],
                                           in1=T[:, q, t, 0:D], op0=ALU.mult, op1=ALU.add).then_inc(a_t1, 1)

                def rectified(t):
                    dve.wait_ge(a_t1, s.times(PAIR, t + 1))
                    v.scalar_tensor_tensor(out=Y[:, slot, t, :], in0=Y[:, slot, t, :], scalar=0.0,
                                           in1=X[:, q, t, :], op0=ALU.max, op1=ALU.add).then_inc(a_y, 1)

                def same_dst(t):
                    if s.exists():
                        dve.wait_ge(a_U, s.times(PAIR, PAIR))
                    dve.wait_ge(a_D, n.times(PAIR, t + 1))
                    v.tensor_scalar(SEL[:, n.slot(2), t, :], PT[t][:, 0:LANES], DCF[:, n.slot(UNROLL), t:t + 1],
                                    None, ALU.is_equal).then_inc(a_sel, 1)

                def dst_wide():
                    r = g.slot(UNROLL)
                    if m.exists():
                        dve.wait_ge(a_D, m.times(PAIR, PAIR))
                    dve.wait_ge(a_idx[r], g.turn(UNROLL, 16 * PAIR, 16 * PAIR))
                    for t in range(PAIR):
                        v.tensor_copy(DB[:, g.slot(2), t, :], wide(IDX[:, r, t, 1:2], LANES))
                    v.tensor_copy(DCF[:, r, :], IDX[:, r, :, 1])
                    old = g.plus(-UNROLL)
                    if old.exists():
                        dve.wait_ge(a_st[old.slot(2)], old.turn(2, 16 * PAIR, 16 * PAIR))
                    v.tensor_tensor(NID[:, r, :], IDX[:, r, :, 2], slot_far[:, :], ALU.add).then_inc(a_prep, 1)

                def low_part(t):
                    dve.wait_ge(a_hi, m.times(PAIR, t + 1))
                    if e.exists():
                        dve.wait_ge(a_z, e.times(PAIR, t + 1))
                    v.tensor_tensor(XL[:, m.slot(2), t, :], PS[t][:, :], XH[:, m.slot(2), t, :].bitcast(f32),
                                    ALU.subtract).then_inc(a_lo, 1)

                def source_stats(t):
                    if t == 0:
                        dve.wait_ge(a_gg[g.slot(UNROLL)], g.turn(UNROLL, 16 * PAIR, 16 * PAIR))
                        if m.exists():
                            dve.wait_ge(a_zg, m.times(PAIR, PAIR))
                    v.bn_stats(gs[0][:, g.slot(2), t, :], G[:, g.slot(2), t, :]).then_inc(a_bn, 1)

                def source_aggr(t):
                    wait_alone(dve, a_bn, g.times(PAIR, t + 1))
                    v.bn_aggr(gs[1][:, g.slot(2), t, :], gs[0][:, g.slot(2), t, :]).then_inc(a_var, 1)

                if s.exists():
                    total(0)
                if e.exists():
                    reciprocal(ys, e, a_ysd, a_yrs)
                if n.exists():
                    reciprocal(gs, n, a_sd, a_rs)
                if m.exists():
                    dve.wait_ge(a_cnt, m.times(1, 1))
                    v.tensor_scalar(CNT[:, m.slot(2), :], CNT[:, m.slot(2), :], 1.0, None, ALU.add).then_inc(a_cnt1, 1)
                if e.exists():
                    minus_mean(ys, e, a_yrs, a_ynm)
                if n.exists():
                    minus_mean(gs, n, a_rs, a_nm)
                    for t in range(PAIR):
                        same_dst(t)
                if g.exists():
                    dst_wide()
                if s.exists():
                    rectified(0)
                if m.exists():
                    low_part(0)
                if s.exists():
                    total(1)
                if m.exists():
                    low_part(1)
                if s.exists():
                    rectified(1)
                if m.exists():
                    dve.wait_ge(a_cnt1, m.times(1, 1))
                    v.reciprocal(RC[:, m.slot(2), :], CNT[:, m.slot(2), :]).then_inc(a_rc, 1)
                if g.exists():
                    source_stats(0)
                if n.exists():
                    dve.wait_ge(a_sel, n.times(PAIR, PAIR))
                    v.reduce_sum(CNT[:, n.slot(2), :], SEL[:, n.slot(2), :, :], AX.X).then_inc(a_cnt, 1)
                if s.exists():
                    y_stats(s, 0, a_y, a_ybn)
                if g.exists():
                    source_stats(1)
                    source_aggr(0)
                if s.exists():
                    y_stats(s, 1, a_y, a_ybn)
                if g.exists():
                    source_aggr(1)
                if s.exists():
                    y_aggr(s, 0, a_ybn, a_yvar)
                if s.exists():
                    y_aggr(s, 1, a_ybn, a_yvar)

            def fast():
                run_steps(dve, NG, 5, 2, step_b)
                dve.wait_ge(b_out, NG * PAIR)
                run_steps(dve, NA, 5, 2, step_a)

            def general():
                def count(at):
                    seen = [0]

                    def then(ins):
                        seen[0] += 1
                        ins.then_inc(g_dve, 1)
                        wait_alone(dve, g_dve, at(seen[0]))
                    return then, seen

                with dve.Fori(0, C) as k:
                    then, seen = count(lambda n: CHUNK_DVE(k, n))
                    dve.wait_ge(g_ld, k * 32 + 32)
                    then(v.tensor_copy(DCF[0:P, 0, 0:1], IDX[0:P, 0, 0, 1:2]))
                    then(v.tensor_copy(DB[0:P, 0, 0, 0:P], wide(IDX[0:P, 0, 0, 1:2], P)))
                    dve.wait_ge(g_gat, k * 16 + 16)
                    then(v.bn_stats(gs[0][0:P, 0, 0, :], G[0:P, 0, 0, :]))
                    then(v.bn_aggr(gs[1][0:P, 0, 0, :], gs[0][0:P, 0, 0, :]))
                    dve.wait_ge(g_act, CHUNK_ACT(k, 1))
                    then(v.reciprocal(gs[3][0:P, 0, 0:1], gs[2][0:P, 0, 0:1]))
                    then(v.scalar_tensor_tensor(out=gs[4][0:P, 0, 0:1], in0=gs[1][0:P, 0, 0, 0:1], scalar=-1.0,
                                                in1=gs[3][0:P, 0, 0:1], op0=ALU.mult, op1=ALU.mult))
                    dve.wait_ge(g_pe, CHUNK_PE(k, 1))
                    then(v.tensor_scalar(SEL[0:P, 0, 0, 0:P], PT[0][0:P, 0:P], DCF[0:P, 0, 0:1], None,
                                         ALU.is_equal))
                    then(v.reduce_sum(S2[0:P, D:D + 1], SEL[0:P, 0, 0, 0:P], AX.X))
                    then(v.tensor_tensor(SEL[0:P, 0, 1, 0:P], SEL[0:P, 0, 0, 0:P], earlier[0:P, 0:P], ALU.mult))
                    then(v.reduce_sum(CNT[0:P, 0, 0:1], SEL[0:P, 0, 1, 0:P], AX.X))
                    then(v.tensor_scalar(CNT[0:P, 0, 0:1], CNT[0:P, 0, 0:1], 0.0, None, ALU.is_gt))
                    then(v.tensor_scalar(RC[0:P, 0, 0:1], lane_no[0:P, :], float(N), None, ALU.add))
                    then(v.tensor_tensor(RC[0:P, 0, 0:1], RC[0:P, 0, 0:1], DCF[0:P, 0, 0:1], ALU.subtract))
                    then(v.tensor_tensor(RC[0:P, 0, 0:1], RC[0:P, 0, 0:1], CNT[0:P, 0, 0:1], ALU.mult))
                    then(v.tensor_tensor(NID[0:P, 0, 0:1], RC[0:P, 0, 0:1], DCF[0:P, 0, 0:1], ALU.add))
                    dve.wait_ge(g_pe, CHUNK_PE(k, 2))
                    then(v.tensor_copy(S2[0:P, 0:D], PL[0][0:P, :]))
                    then(v.memset(SEL[0:P, 0, 1, 0:P], 0.0))
                    assert seen[0] == EDGE_DVE

                def tile(i):
                    then, seen = count(lambda n: TILE_DVE(i, n))
                    dve.wait_ge(g_in, i * 32 + 32)
                    then(v.bn_stats(xs[0][:, 0, 0, :], X[:, 0, 0, :]))
                    then(v.bn_aggr(xs[1][:, 0, 0, :], xs[0][:, 0, 0, :]))
                    then(v.tensor_scalar(CNT[:, 0, 0:1], S2[:, D:D + 1], 1.0, None, ALU.max))
                    then(v.reciprocal(RC[:, 0, 0:1], CNT[:, 0, 0:1]))
                    then(v.tensor_scalar(CNT[:, 0, 1:2], S2[:, D:D + 1], 1.0, None, ALU.min))
                    then(v.tensor_scalar(ZG[:, 0, 0, :], S2[:, 0:D], RC[:, 0, 0:1], None, ALU.mult))
                    dve.wait_ge(g_act, TILE_ACT(i, 1))
                    then(v.reciprocal(xs[3][:, 0, 0:1], xs[2][:, 0, 0:1]))
                    then(v.scalar_tensor_tensor(out=xs[4][:, 0, 0:1], in0=xs[1][:, 0, 0, 0:1], scalar=-1.0,
                                                in1=xs[3][:, 0, 0:1], op0=ALU.mult, op1=ALU.mult))
                    dve.wait_ge(g_act, TILE_ACT(i, 3))
                    v.tensor_tensor(XL[:, 0, 0, :], PT[0][:, :], XH[:, 0, 0, :].bitcast(f32), ALU.subtract)
                    then(v.tensor_tensor(SL[:, :], PS[0][:, :], SH[:, :].bitcast(f32),
                                         ALU.subtract))
                    dve.wait_ge(g_pe, TILE_PE(i, 2))
                    then(v.tensor_tensor(Y[:, 0, 0, :], PL[0][:, :], bias_r[:, :], ALU.add))
                    then(v.scalar_tensor_tensor(out=Y[:, 0, 0, :], in0=bias_l[:, :], scalar=CNT[:, 0, 1:2],
                                                in1=Y[:, 0, 0, :], op0=ALU.mult, op1=ALU.add))
                    then(v.scalar_tensor_tensor(out=Y[:, 0, 0, :], in0=Y[:, 0, 0, :], scalar=0.0,
                                                in1=X[:, 0, 0, :], op0=ALU.max, op1=ALU.add))
                    then(v.bn_stats(ys[0][:, 0, 0, :], Y[:, 0, 0, :]))
                    then(v.bn_aggr(ys[1][:, 0, 0, :], ys[0][:, 0, 0, :]))
                    dve.wait_ge(g_act, TILE_ACT(i, 4))
                    then(v.reciprocal(ys[3][:, 0, 0:1], ys[2][:, 0, 0:1]))
                    then(v.scalar_tensor_tensor(out=ys[4][:, 0, 0:1], in0=ys[1][:, 0, 0, 0:1], scalar=-1.0,
                                                in1=ys[3][:, 0, 0:1], op0=ALU.mult, op1=ALU.mult))
                    assert seen[0] == T_DVE

                with dve.Fori(0, NT - 1) as i:
                    tile(i)
                tile(NT - 1)

            when_fast(dve, fast, general)

        @block.scalar
        def _(act):
            a = nc.scalar

            def sqrt(sd, mv, slot, eps, ready, value, done):
                act.wait_ge(ready, value)
                a.activation(sd[:, slot, :], mv[:, slot, :, 1], ACT.Sqrt, bias=eps[:, 0:1]).then_inc(done, 1)

            def normalized(to, rows, st, slot, t):
                return a.activation(to, rows, ACT.Identity, bias=st[4][:, slot, t:t + 1],
                                    scale=st[3][:, slot, t:t + 1])

            def step_b(s):
                m = s.plus(1)
                if m.exists():
                    for t in range(PAIR):
                        act.wait_ge(b_T, m.times(PAIR, t + 1))
                        if s.plus(-1).exists():
                            act.wait_ge(b_z, s.plus(-1).times(PAIR, t + 1))
                        a.activation(XT[:, m.slot(2), t, :], PT[t][:, :], ACT.Identity).then_inc(b_xt, 1)
                        a.activation(XH[:, m.slot(2), t, :], PT[t][:, :], ACT.Identity).then_inc(b_hi, 1)
                n, e, y = s.plus(2), s.plus(-1), s.plus(-2)
                if n.exists():
                    sqrt(xs[2], xs[1], n.slot(2), eps1, b_var, n.times(PAIR, PAIR), b_sd)
                if y.exists():
                    act.wait_ge(b_ynm, y.times(1, 1))
                    if y.plus(-2).exists():
                        act.wait_ge(b_st[y.slot(2)], y.turn(2, 16))
                    for t in range(PAIR):
                        normalized(O[:, y.slot(2), t, :], Y[:, y.slot(2), t, :], ys, y.slot(2), t).then_inc(b_out, 1)
                if e.exists():
                    sqrt(ys[2], ys[1], e.slot(2), eps4, b_yvar, e.times(PAIR, PAIR), b_ysd)
                if n.exists():
                    act.wait_ge(b_nm, n.times(1, 1))
                    if s.exists():
                        act.wait_ge(b_T, s.times(PAIR, PAIR))
                    for t in range(PAIR):
                        normalized(ZX[:, n.slot(2), t, :], X[:, n.slot(UNROLL), t, :], xs, n.slot(UNROLL),
                                   t).then_inc(b_zn, 1)

            def step_a(s):
                y, e, m, n = s.plus(-2), s.plus(-1), s.plus(1), s.plus(2)
                if e.exists():
                    sqrt(ys[2], ys[1], e.slot(2), eps4, a_yvar, e.times(PAIR, PAIR), a_ysd)
                if n.exists():
                    sqrt(gs[2], gs[1], n.slot(2), eps1, a_var, n.times(PAIR, PAIR), a_sd)
                if y.exists():
                    act.wait_ge(a_ynm, y.times(1, 1))
                    if y.plus(-2).exists():
                        act.wait_ge(a_st[y.slot(2)], y.turn(2, 16 * PAIR))
                    elif y.at == 0:
                        b_done(act)
                    for t in range(PAIR):
                        normalized(O[:, y.slot(2), t, :], Y[:, y.slot(2), t, :], ys, y.slot(2), t).then_inc(a_out, 1)
                if m.exists():
                    for t in range(PAIR):
                        act.wait_ge(a_U, m.times(PAIR, t + 1))
                        if e.exists():
                            act.wait_ge(a_z, e.times(PAIR, t + 1))
                        a.activation(XH[:, m.slot(2), t, :], PS[t][:, :], ACT.Identity).then_inc(a_hi, 1)
                if n.exists():
                    q = n.slot(UNROLL)
                    if s.exists():
                        act.wait_ge(a_U, s.times(PAIR, PAIR))
                    act.wait_ge(a_gx[q], n.turn(UNROLL, 16 * PAIR, 16 * PAIR))
                    act.wait_ge(a_gt[q], n.turn(UNROLL, 16 * PAIR, 16 * PAIR))
                    act.wait_ge(a_nm, n.times(1, 1))
                    for t in range(PAIR):
                        normalized(ZG[:, n.slot(2), t, :], G[:, n.slot(2), t, :], gs, n.slot(2), t).then_inc(a_zg, 1)
                        a.activation(ZX[:, n.slot(2), t, :], X[:, q, t, :], ACT.Identity, bias=T[:, q, t, D + 1:D + 2],
                                     scale=T[:, q, t, D:D + 1]).then_inc(a_zx, 1)

            def fast():
                run_steps(act, NG, 5, 2, step_b)
                act.wait_ge(b_z, NG * PAIR)
                run_steps(act, NA, 5, 2, step_a)

            def general():
                with act.Fori(0, C) as k:
                    act.wait_ge(g_dve, CHUNK_DVE(k, 4))
                    a.activation(gs[2][0:P, 0, 0:1], gs[1][0:P, 0, 0, 1:2], ACT.Sqrt,
                                 bias=eps1[0:P, 0:1]).then_inc(g_act, 1)
                    act.wait_ge(g_dve, CHUNK_DVE(k, 6))
                    a.activation(ZG[0:P, 0, 0, :], G[0:P, 0, 0, :], ACT.Identity, bias=gs[4][0:P, 0, 0:1],
                                 scale=gs[3][0:P, 0, 0:1]).then_inc(g_act, 1)

                def tile(i):
                    act.wait_ge(g_dve, TILE_DVE(i, 2))
                    a.activation(xs[2][:, 0, 0:1], xs[1][:, 0, 0, 1:2], ACT.Sqrt, bias=eps1[:, 0:1]).then_inc(g_act, 1)
                    act.wait_ge(g_dve, TILE_DVE(i, 8))
                    normalized(ZX[:, 0, 0, :], X[:, 0, 0, :], xs, 0, 0).then_inc(g_act, 1)
                    act.wait_ge(g_pe, TILE_PE(i, 1))
                    a.activation(XH[:, 0, 0, :], PT[0][:, :], ACT.Identity)
                    a.activation(SH[:, :], PS[0][:, :], ACT.Identity).then_inc(g_act, 1)
                    act.wait_ge(g_dve, TILE_DVE(i, 14))
                    a.activation(ys[2][:, 0, 0:1], ys[1][:, 0, 0, 1:2], ACT.Sqrt, bias=eps4[:, 0:1]).then_inc(g_act, 1)
                    act.wait_ge(g_dve, TILE_DVE(i, 16))
                    normalized(O[:, 0, 0, :], Y[:, 0, 0, :], ys, 0, 0).then_inc(g_act, 1)

                with act.Fori(0, NT - 1) as i:
                    tile(i)
                tile(NT - 1)

            when_fast(act, fast, general)

        @block.tensor
        def _(pe):
            m_ = nc.tensor

            def chunk(b, k):
                return b[:, k * LANES:(k + 1) * LANES]

            def product(bank, hi, lo, w_hi, w_lo, wait_hi, wait_lo, start=True, stop=True):
                wait_hi()
                for k in range(KC):
                    m_.matmul(bank, chunk(hi, k), w_hi[:, k, :], start=start and k == 0, stop=False)
                    m_.matmul(bank, chunk(hi, k), w_lo[:, k, :], start=False, stop=False)
                wait_lo()
                for k in range(KC):
                    last = m_.matmul(bank, chunk(lo, k), w_hi[:, k, :], start=False, stop=stop and k == KC - 1)
                return last

            pe.wait_ge(s_const, 1)
            pe.wait_ge(s_viol, 1)
            m_.matmul(PT[0][0:1, 0:1], v_sum[:, :], ones[0:P, 0:1], start=True, stop=True).then_inc(s_flagp, 1)
            pe.wait_ge(s_w, 32)
            for w, full in enumerate((G, ZG)):
                for k in range(KC):
                    bank = (PS, PL, PR, PT)[k][w]
                    if bank is PT[0]:
                        pe.wait_ge(s_flag, 1)
                    for o in range(KC):
                        last = m_.transpose(chunk(bank, o), chunk(full[:, o // PAIR, o % PAIR, :], k), ident[:, :])
                    last.then_inc(s_wT, 1)
            pe.wait_ge(s_wdone, 2 * KC)
            for k in range(KC):
                m_.matmul(PS[0][:, :], bwide[:, k, :], Y[:, k // PAIR, k % PAIR, :], start=k == 0, stop=k == KC - 1)
            for k in range(KC):
                m_.matmul(PL[0][:, :], bwide[:, k, :], O[:, k // PAIR, k % PAIR, :], start=k == 0, stop=False)
            m_.matmul(PL[0][:, :], ones[0:1, :], blrow[0:1, :], start=False, stop=True).then_inc(s_bias, 1)

            def transposed(bank, rows):
                for k in range(KC):
                    last = m_.transpose(chunk(bank, k), chunk(rows, k), ident[:, :])
                return last

            def step_b(s):
                n = s.plus(1)
                if n.exists():
                    for t in range(PAIR):
                        pe.wait_ge(b_zn, n.times(PAIR, t + 1))
                        if s.exists():
                            pe.wait_ge(b_hi, s.times(PAIR, t + 1))
                        transposed(PT[t], ZX[:, n.slot(2), t, :]).then_inc(b_T, 1)
                if s.exists():
                    for t in range(PAIR):
                        if s.plus(-2).exists():
                            pe.wait_ge(b_t, s.plus(-2).times(PAIR, t + 1))
                        product(PZ[s.slot(2)][t][:, :], XH[:, s.slot(2), t, :], XL[:, s.slot(2), t, :], ws_hi, ws_lo,
                                lambda: pe.wait_ge(b_hi, s.times(PAIR, t + 1)),
                                lambda: pe.wait_ge(b_lo, s.times(PAIR, t + 1))).then_inc(b_z, 1)

            def step_a(s):
                m, n, g = s.plus(1), s.plus(2), s.plus(3)
                for t in range(PAIR):
                    if m.exists():
                        pe.wait_ge(a_sel, m.times(PAIR, t + 1))
                        pe.wait_ge(a_zg, m.times(PAIR, t + 1))
                        pe.wait_ge(a_zx, m.times(PAIR, t + 1))
                        if s.exists():
                            pe.wait_ge(a_lo, s.times(PAIR, t + 1))
                        for k in range(KC):
                            m_.matmul(chunk(PS[t], k), chunk(ZG[:, m.slot(2), t, :], k),
                                      SEL[:, m.slot(2), t, :], start=True, stop=False)
                            last = m_.matmul(chunk(PS[t], k), chunk(ZX[:, m.slot(2), t, :], k),
                                             SEL[:, m.slot(2), t, :], start=False, stop=True)
                        last.then_inc(a_U, 1)
                    if s.exists():
                        if s.plus(-2).exists():
                            pe.wait_ge(a_t1, s.plus(-2).times(PAIR, t + 1))
                        product(PZ[s.slot(2)][t][:, :], XH[:, s.slot(2), t, :], XL[:, s.slot(2), t, :], wl_hi, wl_lo,
                                lambda: pe.wait_ge(a_hi, s.times(PAIR, t + 1)),
                                lambda: pe.wait_ge(a_lo, s.times(PAIR, t + 1))).then_inc(a_z, 1)
                if g.exists():
                    pe.wait_ge(a_prep, g.times(1, 1))
                    for t in range(PAIR):
                        if n.exists():
                            pe.wait_ge(a_sel, n.times(PAIR, t + 1))
                        m_.transpose(PT[t][:, 0:LANES], DB[:, g.slot(2), t, :], ident[:, :]).then_inc(a_D, 1)

            def fast():
                pe.wait_ge(s_setup, 1)
                run_steps(pe, NG, 5, 2, step_b)
                pe.wait_ge(b_hi, NG * PAIR)
                pe.wait_ge(b_t, NG * PAIR)
                run_steps(pe, NA, 5, 2, step_a)

            def general():
                pe.wait_ge(s_setup, 1)
                with pe.Fori(0, C) as k:
                    pe.wait_ge(g_dve, CHUNK_DVE(k, 2))
                    m_.matmul(PT[0][0:P, 0:P], DB[0:P, 0, 0, 0:P], ident[0:P, 0:P],
                              start=True, stop=True).then_inc(g_pe, 1)
                    pe.wait_ge(g_dve, CHUNK_DVE(k, 7))
                    pe.wait_ge(g_act, CHUNK_ACT(k, 2))
                    m_.matmul(PL[0][0:P, :], SEL[0:P, 0, 0, 0:P], ZG[0:P, 0, 0, :],
                              start=True, stop=True).then_inc(g_pe, 1)

                def tile(i):
                    pe.wait_ge(g_dve, TILE_DVE(i, 8))
                    pe.wait_ge(g_act, TILE_ACT(i, 2))
                    transposed(PT[0], ZX[:, 0, 0, :])
                    transposed(PS[0], ZG[:, 0, 0, :]).then_inc(g_pe, 1)
                    pe.wait_ge(g_dve, TILE_DVE(i, 9))
                    ready = lambda: None
                    product(PL[0][:, :], XH[:, 0, 0, :], XL[:, 0, 0, :], wr_hi, wr_lo, ready, ready, stop=False)
                    product(PL[0][:, :], SH[:, :], SL[:, :], wl_hi, wl_lo, ready, ready,
                            start=False).then_inc(g_pe, 1)

                with pe.Fori(0, NT - 1) as i:
                    tile(i)
                tile(NT - 1)

            when_fast(pe, fast, general)


_INS = ["x", "src", "dst", "L0_gnn_W_l", "L0_gnn_b_l", "L0_gnn_W_r", "L0_gnn_gamma", "L0_gnn_beta"]


def kernel(**inputs):
    import numpy as _np
    import concourse.bacc as _bacc
    from concourse import mybir as _mybir
    from concourse.bass_utils import run_bass_kernel_spmd as _run

    nc = _bacc.Bacc("TRN2", target_bir_lowering=False, num_devices=1)
    arrays, args = {}, []
    for name in _INS:
        a = _np.ascontiguousarray(inputs[name])
        arrays[f"in_{name}"] = a
        args.append(nc.dram_tensor(f"in_{name}", a.shape, _mybir.dt.from_np(a.dtype), kind="ExternalInput").ap())
    shape = arrays["in_x"].shape
    result = nc.dram_tensor("result", shape, _mybir.dt.float32, kind="ExternalOutput").ap()
    gnn_kernel(nc, *args, result)
    r = _run(nc, [arrays], core_ids=[0])
    return r.results[0]["result"]
```

```python
import concourse.bass as bass
from concourse import mybir
from contextlib import ExitStack

LANES = 128
PAIR = 2
UNROLL = 6
WINDOW = 128
STRIDE = 123
RUN = WINDOW - STRIDE + 1
FAR = 1 << 20


class Step:

    def __init__(self, at, total, reg=None):
        self.at, self.total, self.reg = at, total, reg

    def plus(self, k):
        return Step(self.at + k, self.total, self.reg)

    def exists(self):
        return self.reg is not None or 0 <= self.at < self.total

    def times(self, m, k):
        if self.reg is None:
            return m * self.at + k
        return self.reg * (m * UNROLL) + (m * self.at + k)

    def slot(self, n):
        return self.at % n

    def turn(self, n, m=1, k=0):
        if self.reg is None:
            return m * (self.at // n) + k
        return self.reg * (m * (UNROLL // n)) + (m * (self.at // n) + k)


def run_steps(eng, total, ahead, behind, body):
    loops = max(total - 1 - ahead - UNROLL, 0) // UNROLL
    for at in range(-ahead, UNROLL):
        body(Step(at, total))
    if loops:
        with eng.Fori(0, loops) as reg:
            for u in range(UNROLL):
                body(Step(UNROLL + u, total, reg))
    for at in range(UNROLL + UNROLL * loops, total + behind):
        body(Step(at, total))


def gnn_kernel(nc, x, src, dst, w_l, b_l, w_r, gamma, beta, out):
    f32, f32r, i32 = mybir.dt.float32, mybir.dt.float32r, mybir.dt.int32
    ALU, ACT, AX = mybir.AluOpType, mybir.ActivationFunctionType, mybir.AxisListType
    N, D = x.shape
    E = src.shape[0]
    KC = D // LANES
    EPS = 1e-5
    GROUP = PAIR * LANES
    NG = -(-N // GROUP)
    P = max(p for p in range(1, LANES + 1) if E % p == 0)
    C = E // P
    MORE = max(E - N, 0)
    NA = max(-(-MORE // (PAIR * STRIDE)), 1)
    ROWS = NA * PAIR * STRIDE + WINDOW
    BODIES = NG // UNROLL
    PER_BODY = -(-C // BODIES)
    QUOTA = [PER_BODY * (u + 1) // UNROLL - PER_BODY * u // UNROLL for u in range(UNROLL)]
    CPAD = PER_BODY * -(-NG // UNROLL)
    SUMW = D + 4
    NT = -(-N // LANES)
    SROWS = LANES * -(-(N + LANES) // LANES)

    DIFFS = KC // 2 * LANES
    STATW = D + 2
    assert C <= D

    dense = nc.dram_tensor("dense_edges", (ROWS, 3), i32, kind="Internal").ap()
    sums = nc.dram_tensor("pass_b_sums", (N, STATW), f32, kind="Internal").ap()
    table = nc.dram_tensor("sum_table", (SROWS, SUMW), f32, kind="Internal").ap()

    ctx = ExitStack()
    with ctx:
        def sb(name, shape, dt=f32):
            return ctx.enter_context(nc.sbuf_tensor(name, shape, dt))

        def sem(name):
            return ctx.enter_context(nc.semaphore(name))

        wl_hi, wl_lo = sb("wl_hi", [LANES, KC, D], f32r), sb("wl_lo", [LANES, KC, D], f32r)
        wr_hi, wr_lo = sb("wr_hi", [LANES, KC, D], f32r), sb("wr_lo", [LANES, KC, D], f32r)
        ws_hi, ws_lo = sb("ws_hi", [LANES, KC, D], f32r), sb("ws_lo", [LANES, KC, D], f32r)
        bias_l, bias_r, bias_s = sb("bias_l", [LANES, D]), sb("bias_r", [LANES, D]), sb("bias_s", [LANES, D])
        ident, ones = sb("ident", [LANES, LANES]), sb("ones", [LANES, LANES])
        eps1, eps4 = sb("eps1", [LANES, 1]), sb("eps4", [LANES, 1])
        X = sb("x_rows", [LANES, UNROLL, PAIR, D])
        G = sb("src_rows", [LANES, 2, PAIR, D])
        ZX = sb("z_rows", [LANES, 2, PAIR, D])
        ZG = sb("z_src", [LANES, 2, PAIR, D])
        XT = sb("z_T", [LANES, 2, PAIR, D])
        T = sb("sums", [LANES, UNROLL, PAIR, STATW])
        XH, XL = sb("z_T_hi", [LANES, 2, PAIR, D], f32r), sb("z_T_lo", [LANES, 2, PAIR, D], f32r)
        SH, SL = sb("mean_T_hi", [LANES, D], f32r), sb("mean_T_lo", [LANES, D], f32r)
        Y = sb("y_rows", [LANES, 2, PAIR, D])
        O = sb("out_rows", [LANES, 2, PAIR, D])
        SEL = sb("same_dst", [LANES, 2, PAIR, LANES])
        DB = sb("dst_wide", [LANES, 2, PAIR, LANES])

        def stats(name, slots=2):
            both = sb(name + "_rs_nm", [LANES, slots, PAIR, 2])
            return (sb(name + "_bn", [LANES, 2, PAIR, 6]), sb(name + "_mv", [LANES, 2, PAIR, 2]),
                    sb(name + "_sd", [LANES, 2, PAIR]), both[:, :, :, 0], both[:, :, :, 1], both, slots)

        xs, gs, ys = stats("xst", UNROLL), stats("gst"), stats("yst")
        IDX = sb("edge_idx", [LANES, UNROLL, PAIR, 3], i32)
        NID = sb("node_idx", [LANES, UNROLL, PAIR], i32)
        DCF = sb("dst_f", [LANES, UNROLL, PAIR])
        CNT, RC = sb("count", [LANES, 2, PAIR]), sb("rcount", [LANES, 2, PAIR])
        slot_far = sb("slot_far", [LANES, PAIR])
        lane_no = sb("lane_no", [LANES, 1])
        earlier = sb("earlier", [LANES, LANES])
        def copy_of_list(i):
            return T[0:P, 2 + i // PAIR, i % PAIR, 0:C]

        e_d, e_s, e_next = (copy_of_list(i).bitcast(i32) for i in range(3))
        e_prev, e_run, e_no = (sb(name, [P, C], i32) for name in ("e_prev", "e_run", "e_no"))
        f_a, f_b, f_v, f_nl = (copy_of_list(i) for i in range(4, 8))
        v_sum = sb("v_sum", [P, 1])
        flag = sb("flag", [1, 1], i32)
        REC = sb("records", [P, CPAD, 4], i32)
        STG = sb("rec_stage", [P, UNROLL, max(QUOTA), 4], i32)
        tail_rec = sb("tail_rec", [1, (ROWS - MORE) * 3], i32)
        gcol, bcol = sb("gamma_col", [LANES, KC]), sb("beta_col", [LANES, KC])
        blrow = sb("bl_row", [1, D])
        S2 = sb("sum_rows", [LANES, SUMW])
        bwide = T[:, 1, 0, 0:D].rearrange("p (k c) -> p k c", c=LANES)

        PT = [ctx.enter_context(nc.psum_tensor(f"pT{t}", [LANES, D], f32)) for t in range(PAIR)]
        PS = [ctx.enter_context(nc.psum_tensor(f"pS{t}", [LANES, D], f32)) for t in range(PAIR)]
        PL = [ctx.enter_context(nc.psum_tensor(f"pL{t}", [LANES, D], f32)) for t in range(PAIR)]
        PR = [ctx.enter_context(nc.psum_tensor(f"pR{t}", [LANES, D], f32)) for t in range(PAIR)]
        PZ = [PL, PR]
        W_BANKS = (PS + PL, PR + PT[::-1])

        s_w, s_edges, s_small = sem("weights_in"), sem("edges_in"), sem("small_in")
        s_pad, s_id0, s_const = sem("edge_pads_set"), sem("ident_zeroed"), sem("constants_set")
        s_wT, s_half, s_raw, s_whi, s_wlo = (
            sem(n) for n in ("weights_T", "gamma_halved", "raw_copied", "weights_hi", "weights_lo"))
        s_bias = sem("bias")
        s_chain, s_viol, s_flagp, s_flag = sem("dve_setup_chain"), sem("violations"), sem("flag_psum"), sem("flag_set")
        s_passed = sem("waits_passed")
        s_tail, s_pool0 = sem("tail_written"), sem("pool_setup_chain")
        b_ld = [sem(f"b_x_in{i}") for i in range(UNROLL)]
        b_st = [sem(f"b_out_stored{i}") for i in range(2)]
        b_ts = [sem(f"b_sums_stored{i}") for i in range(2)]
        b_bn, b_var, b_sd, b_rs, b_nm = (sem("b_x_" + n) for n in ("bn", "var", "sd", "rs", "nm"))
        b_zn, b_T, b_hi, b_lo, b_z = (sem("b_" + n) for n in ("z_rows", "z_T_psum", "hi", "lo", "product"))
        b_t, b_y, b_ybn, b_yvar, b_ysd, b_yrs, b_ynm, b_out = (
            sem("b_" + n) for n in ("biased", "y", "y_bn", "y_var", "y_sd", "y_rs", "y_nm", "out"))
        b_stage = sem("b_records_staged")
        b_sc = [sem(f"b_scattered{i}") for i in range(UNROLL)]
        a_idx = [sem(f"a_idx_in{i}") for i in range(UNROLL)]
        a_gx = [sem(f"a_x_gathered{i}") for i in range(UNROLL)]
        a_gg = [sem(f"a_src_gathered{i}") for i in range(UNROLL)]
        a_gt = [sem(f"a_sums_gathered{i}") for i in range(UNROLL)]
        a_st = [sem(f"a_out_scattered{i}") for i in range(2)]
        a_bn, a_var, a_sd, a_rs, a_nm = (sem("a_in_" + n) for n in ("bn", "var", "sd", "rs", "nm"))
        a_prep, a_D, a_sel, a_cnt, a_cnt1, a_rc = (
            sem("a_" + n) for n in ("dst_ready", "dst_psum", "same_dst", "count_psum", "count", "rcount"))
        a_diff, a_wide = sem("a_z_differences"), sem("a_dst_wide")
        a_zx, a_zg, a_U, a_hi, a_lo, a_z = (
            sem("a_" + n) for n in ("z_rows", "z_src", "diff_sum_T", "hi", "lo", "product"))
        a_t1, a_y, a_ybn, a_yvar, a_ysd, a_yrs, a_ynm, a_out = (
            sem("a_" + n) for n in ("total", "y", "y_bn", "y_var", "y_sd", "y_rs", "y_nm", "out"))
        g_zero, g_ld, g_gat, g_add = sem("g_zeroed"), sem("g_edges_in"), sem("g_gathered"), sem("g_added")
        g_dve, g_act, g_pe = sem("g_dve"), sem("g_act"), sem("g_pe")
        g_in, g_st = sem("g_rows_in"), sem("g_stored")
        g_wT, g_raw, g_whi, g_wlo, g_bias, g_setup = (
            sem("g_" + n) for n in ("weights_T", "raw_copied", "weights_hi", "weights_lo", "bias_psum", "setup_done"))

        block = ctx.enter_context(nc.Block())

        def wide(ap, n):
            return ap.to_broadcast([ap.shape[0], n])

        def node_rows(dram, s):
            if s.reg is None:
                base = min(s.at * GROUP, N - GROUP)
                rows = dram[base:base + GROUP, :]
            else:
                rows = dram[bass.ds(s.times(GROUP, 0), GROUP), :]
            return rows.rearrange("(p t) d -> p t d", t=PAIR)

        def windows(s):
            def one(t):
                if s.reg is None:
                    b = s.at * PAIR * STRIDE + t * STRIDE
                    return dense[b:b + WINDOW, :]
                return dense[bass.ds(s.times(PAIR * STRIDE, t * STRIDE), WINDOW), :]
            return [one(t) for t in range(PAIR)]

        def all_stored(eng, stores):
            for i in range(2):
                eng.wait_ge(stores[i], 16 * len(range(i, NG, 2)))

        def scatters(i):
            return PER_BODY * (i // UNROLL) + sum(QUOTA[:i % UNROLL]) < C

        def wait_alone(eng, semaphore, value):
            eng.wait_ge(semaphore, value)
            eng.sem_inc(s_passed, 1)

        def when_fast(eng, fast, general):
            eng.wait_ge(s_flag, 1)
            bad = eng.value_load(flag[0:1, 0:1], min_val=0, max_val=4 * E)
            with eng.If(bad == 0):
                fast()
            with eng.Else():
                general()

        EDGE_DVE, EDGE_ACT, EDGE_PE = 17, 2, 2
        T_DVE, T_ACT, T_PE = 16, 5, 2

        def CHUNK_DVE(k, n):
            return k * EDGE_DVE + n

        def CHUNK_ACT(k, n):
            return k * EDGE_ACT + n

        def CHUNK_PE(k, n):
            return k * EDGE_PE + n

        def TILE_DVE(i, n):
            return i * T_DVE + (C * EDGE_DVE + n)

        def TILE_ACT(i, n):
            return i * T_ACT + (C * EDGE_ACT + n)

        def TILE_PE(i, n):
            return i * T_PE + (C * EDGE_PE + n)

        @block.sync
        def _(sp):
            sp.dma_start(e_d[:, :], dst.rearrange("(p c) -> p c", c=C)).then_inc(s_edges, 16)
            sp.dma_start(e_s[:, :], src.rearrange("(p c) -> p c", c=C)).then_inc(s_edges, 16)
            sp.wait_ge(s_pad, 1)
            for shifted, k in ((e_next, 1), (e_run, RUN + 1)):
                sp.dma_start(shifted[0:P - 1, :],
                             dst[k:k + (P - 1) * C].rearrange("(p c) -> p c", c=C)).then_inc(s_edges, 16)
                sp.dma_start(shifted[P - 1:P, 0:C - k],
                             dst[k + (P - 1) * C:E].rearrange("(p c) -> p c", p=1)).then_inc(s_edges, 16)
            sp.dma_start(e_prev[1:P, :], dst[C - 1:E - 1].rearrange("(p c) -> p c", c=C)).then_inc(s_edges, 16)
            sp.dma_start(e_prev[0:1, 1:C], dst[0:C - 1].rearrange("(p c) -> p c", p=1)).then_inc(s_edges, 16)
            sp.dma_start(G[:, :, :, :].rearrange("p a b d -> p (a b) d"),
                         w_l.rearrange("(k p) i -> p k i", p=LANES)).then_inc(s_w, 16)
            sp.dma_start(ZG[:, :, :, :].rearrange("p a b d -> p (a b) d"),
                         w_r.rearrange("(k p) i -> p k i", p=LANES)).then_inc(s_w, 16)
            sp.dma_start(gcol[:, :], gamma.rearrange("(k p) -> p k", p=LANES),
                         allow_slow_non_contiguous=True).then_inc(s_small, 16)
            sp.dma_start(bcol[:, :], beta.rearrange("(k p) -> p k", p=LANES),
                         allow_slow_non_contiguous=True).then_inc(s_small, 16)
            sp.dma_start(blrow[0:1, :], b_l.rearrange("(a d) -> a d", a=1)).then_inc(s_small, 16)

            def b_load(s):
                if s.plus(-UNROLL).exists():
                    sp.wait_ge(b_y, s.plus(-UNROLL).times(PAIR, PAIR))
                sp.dma_start(X[:, s.slot(UNROLL), :, :], node_rows(x, s)).then_inc(b_ld[s.slot(UNROLL)], 16)

            def b_store_sums(s):
                sp.wait_ge(b_t, s.times(PAIR, PAIR))
                if s.at == NG - 1:
                    sp.wait_ge(b_ts[s.plus(-1).slot(2)], s.plus(-1).turn(2, 16, 16))
                sp.dma_start(node_rows(sums, s), T[:, s.slot(2), :, :]).then_inc(b_ts[s.slot(2)], 16)

            def b_store(s):
                sp.wait_ge(b_out, s.times(PAIR, PAIR))
                if s.at == NG - 1:
                    sp.wait_ge(b_st[s.plus(-1).slot(2)], s.plus(-1).turn(2, 16, 16))
                sp.dma_start(node_rows(out, s), O[:, s.slot(2), :, :]).then_inc(b_st[s.slot(2)], 16)

            def a_load(n):
                old = n.plus(-UNROLL)
                if old.exists():
                    for done in (a_gx, a_gg, a_gt):
                        wait_alone(sp, done[n.slot(UNROLL)], n.turn(UNROLL, 16 * PAIR))
                    wait_alone(sp, a_wide, old.times(PAIR, PAIR))
                    wait_alone(sp, a_prep, old.times(1, 1))
                for t, rows in enumerate(windows(n)):
                    sp.dma_start(IDX[:, n.slot(UNROLL), t, :], rows).then_inc(a_idx[n.slot(UNROLL)], 16)

            def step_b(s):
                if s.plus(5).exists():
                    b_load(s.plus(5))
                if s.plus(-2).exists():
                    b_store(s.plus(-2))
                if s.exists():
                    b_store_sums(s)
                if s.at == NG - 4 and s.reg is None:
                    sp.wait_ge(s_tail, 16)
                    for u in range(UNROLL):
                        sp.wait_ge(b_sc[u], 16 * QUOTA[u] * len([i for i in range(u, NG, UNROLL) if scatters(i)]))
                    for n in range(min(5, NA)):
                        a_load(Step(n, NA))

            def step_a(s):
                n = s.plus(5)
                if n.exists() and (s.reg is not None or s.at >= 0):
                    a_load(n)

            def fast():
                sp.wait_ge(s_pool0, 2)
                sp.dma_start(dense[MORE:ROWS, :].rearrange("(a r) c -> a (r c)", a=1),
                             tail_rec[0:1, :]).then_inc(s_tail, 16)
                run_steps(sp, NG, 5, 2, step_b)
                run_steps(sp, NA, 5, 2, step_a)
                for i in range(2):
                    sp.wait_ge(a_st[i], 16 * PAIR * len(range(i, NA, 2)))

            def general():
                sp.wait_ge(s_viol, 2)
                sp.wait_ge(s_pool0, 2)
                zero = S2[:, :]
                with sp.Fori(0, SROWS // LANES) as i:
                    sp.dma_start(table[bass.ds(i * LANES, LANES), :], zero).then_inc(g_zero, 16)
                sp.wait_ge(g_zero, 16 * (SROWS // LANES))
                with sp.Fori(0, C) as k:
                    sp.dma_start(IDX[0:P, 0, 0, 0:1],
                                 src[bass.ds(k * P, P)].rearrange("(p c) -> p c", c=1)).then_inc(g_ld, 16)
                    sp.dma_start(IDX[0:P, 0, 0, 1:2],
                                 dst[bass.ds(k * P, P)].rearrange("(p c) -> p c", c=1)).then_inc(g_ld, 16)
                    wait_alone(sp, g_add, k * 16 + 16)

                def tile(i, base):
                    sp.dma_start(X[:, 0, 0, :], x[base, :]).then_inc(g_in, 16)
                    sp.dma_start(S2[:, :], table[base, :]).then_inc(g_in, 16)
                    sp.wait_ge(g_act, TILE_ACT(i, 5))
                    sp.dma_start(out[base, :], O[:, 0, 0, :]).then_inc(g_st, 16)
                    wait_alone(sp, g_st, i * 16 + 16)

                with sp.Fori(0, NT - 1) as i:
                    tile(i, bass.ds(i * LANES, LANES))
                tile(NT - 1, slice(N - LANES, N))

            when_fast(sp, fast, general)

        @block.gpsimd
        def _(pool):
            pool.memset(ident[:, :], 0.0).then_inc(s_id0, 1)
            pool.memset(ones[:, :], 1.0)
            pool.memset(earlier[:, :], 1.0).then_inc(s_id0, 1)
            pool.wait_ge(s_id0, 2)
            pool.affine_select(out=ident[:, :], in_=ident[:, :], compare_op=ALU.not_equal, fill=1.0,
                               base=0, pattern=[[-1, LANES]], channel_multiplier=1)
            pool.affine_select(out=earlier[:, :], in_=earlier[:, :], compare_op=ALU.is_gt, fill=0.0,
                               base=0, pattern=[[-1, LANES]], channel_multiplier=1)
            pool.iota(e_no[:, :], pattern=[[1, C]], base=0, channel_multiplier=C)
            pool.iota(IDX[:, 0, 0, 0:1], pattern=[[0, 1]], base=0, channel_multiplier=1).then_inc(s_const, 1)
            pool.memset(tail_rec[:, :], FAR)
            pool.memset(STG[:, :, :, :], 0).then_inc(s_pool0, 1)
            pool.memset(S2[:, :], 0.0).then_inc(s_pool0, 1)
            pool.wait_ge(s_viol, 2)
            pool.memset(T[:, 2:, :, :], 0.0).then_inc(s_pool0, 1)

            def b_scatter(s):
                q, u = QUOTA[s.slot(UNROLL)], s.slot(UNROLL)
                if not q or s.reg is None and not scatters(s.at):
                    return
                col = s.turn(UNROLL, PER_BODY, sum(QUOTA[:u]))
                if s.plus(-UNROLL).exists():
                    pool.wait_ge(b_sc[u], s.turn(UNROLL, 16 * q))
                cols = slice(col, col + q) if s.reg is None else bass.ds(col, q)
                pool.tensor_copy(STG[:, u, 0:q, :], REC[:, cols, :]).then_inc(b_stage, 1)
                wait_alone(pool, b_stage, s.times(1, 1))
                for j in range(q):
                    pool.indirect_dma_start(
                        out=dense[:, :], out_offset=bass.IndirectOffsetOnAxis(ap=STG[:, u, j, 3:4], axis=0),
                        in_=STG[:, u, j, 0:3], in_offset=None,
                        bounds_check=ROWS - 1, oob_is_err=False).then_inc(b_sc[u], 16)

            def step_b(s):
                if s.exists():
                    b_scatter(s)
                n = s.plus(1)
                if n.exists():
                    for t in range(PAIR):
                        pool.wait_ge(b_hi, n.times(PAIR, t + 1))
                        if s.plus(-1).exists():
                            pool.wait_ge(b_z, s.plus(-1).times(PAIR, t + 1))
                        pool.tensor_tensor(XL[:, n.slot(2), t, :], XT[:, n.slot(2), t, :],
                                           XH[:, n.slot(2), t, :].bitcast(f32), ALU.subtract).then_inc(b_lo, 1)

            def gather(to, rows, idx, done):
                pool.indirect_dma_start(out=to, out_offset=None, in_=rows,
                                        in_offset=bass.IndirectOffsetOnAxis(ap=idx, axis=0),
                                        bounds_check=N - 1, oob_is_err=False).then_inc(done, 16)

            def gather_rows(n):
                q = n.slot(UNROLL)
                pool.wait_ge(a_idx[q], n.turn(UNROLL, 16 * PAIR, 16 * PAIR))
                if n.plus(-UNROLL).exists():
                    wait_alone(pool, a_y, n.plus(-UNROLL).times(PAIR, PAIR))
                for t in range(PAIR):
                    gather(X[:, q, t, :], x[:, :], IDX[:, q, t, 1:2], a_gx[q])

            def gather_sources(n):
                q = n.slot(UNROLL)
                if n.plus(-2).exists():
                    wait_alone(pool, a_zg, n.plus(-2).times(PAIR, PAIR))
                for t in range(PAIR):
                    gather(G[:, n.slot(2), t, :], x[:, :], IDX[:, q, t, 0:1], a_gg[q])

            def gather_sums(n):
                q = n.slot(UNROLL)
                if n.plus(-UNROLL).exists():
                    wait_alone(pool, a_t1, n.plus(-UNROLL).times(PAIR, PAIR))
                for t in range(PAIR):
                    gather(T[:, q, t, :], sums[:, :], IDX[:, q, t, 1:2], a_gt[q])

            EARLY = min(2, NA)

            def step_a(s):
                n, y = s.plus(4), s.plus(-2)
                if n.exists() and (s.reg is not None or n.at >= EARLY):
                    gather_rows(n)
                    gather_sums(n)
                if y.exists():
                    for t in range(PAIR):
                        wait_alone(pool, a_out, y.times(PAIR, t + 1))
                        pool.indirect_dma_start(
                            out=out[:, :], out_offset=bass.IndirectOffsetOnAxis(ap=NID[:, y.slot(UNROLL), t:t + 1], axis=0),
                            in_=O[:, y.slot(2), t, :], in_offset=None,
                            bounds_check=N - 1, oob_is_err=False).then_inc(a_st[y.slot(2)], 16)
                if n.exists() and (s.reg is not None or n.at >= EARLY):
                    gather_sources(n)

            def fast():
                pool.wait_ge(s_viol, 2)
                run_steps(pool, NG, 5, 2, step_b)
                for n in range(EARLY):
                    wait_alone(pool, a_idx[n], 16 * PAIR)
                    gather_sources(Step(n, NA))
                    last = max(i for i in range(NG) if i % UNROLL == n)
                    wait_alone(pool, b_y, last * PAIR + PAIR)
                    gather_rows(Step(n, NA))
                pool.wait_ge(b_y, NG * PAIR)
                all_stored(pool, b_ts)
                for n in range(EARLY):
                    gather_sums(Step(n, NA))
                run_steps(pool, NA, 5, 2, step_a)

            def general():
                pool.wait_ge(g_setup, 1)
                with pool.Fori(0, C) as k:
                    wait_alone(pool, g_ld, k * 32 + 32)
                    gather(G[0:P, 0, 0, :], x[:, :], IDX[0:P, 0, 0, 0:1], g_gat)
                    wait_alone(pool, g_dve, CHUNK_DVE(k, EDGE_DVE))
                    pool.indirect_dma_start(
                        out=table[:, :], out_offset=bass.IndirectOffsetOnAxis(ap=NID[0:P, 0, 0:1], axis=0),
                        in_=S2[0:P, :], in_offset=None, bounds_check=SROWS - 1, oob_is_err=True,
                        compute_op=ALU.add).then_inc(g_add, 16)

            when_fast(pool, fast, general)

        @block.vector
        def _(dve):
            v = nc.vector
            links = [0]

            def link(ins):
                links[0] += 1
                ins.then_inc(s_chain, 1)
                dve.wait_ge(s_chain, links[0])

            v.memset(e_next[:, :], N)
            v.memset(e_prev[:, :], -1)
            v.memset(e_run[:, :], N).then_inc(s_pad, 1)
            v.memset(eps1[:, :], EPS)
            v.memset(eps4[:, :], EPS / 4)
            v.memset(REC[:, :, :], FAR)
            dve.wait_ge(s_edges, 16 * 8)
            dve.wait_ge(s_const, 1)
            link(v.tensor_tensor(f_a[:, :], e_next[:, :], e_d[:, :], ALU.subtract))
            v.tensor_scalar(f_nl[:, :], f_a[:, :], 0.0, None, ALU.is_equal)
            link(v.tensor_tensor(f_b[:, :], e_s[:, :], e_d[:, :], ALU.is_equal))
            link(v.scalar_tensor_tensor(out=f_b[:, :], in0=f_a[:, :], scalar=1.0, in1=f_b[:, :],
                                        op0=ALU.is_equal, op1=ALU.mult))
            v.tensor_tensor(f_v[:, :], e_run[:, :], e_d[:, :], ALU.is_equal)
            link(v.tensor_tensor(f_b[:, :], f_b[:, :], f_nl[:, :], ALU.add))
            link(v.tensor_tensor(f_v[:, :], f_v[:, :], f_b[:, :], ALU.subtract))
            link(v.reduce_sum(v_sum[:, :], f_v[:, :], AX.X))
            link(v.tensor_scalar(v_sum[:, :], v_sum[:, :], float(C), None, ALU.add))
            link(v.tensor_scalar(f_b[0:1, 0:1], e_d[0:1, 0:1], 0.0, None, ALU.not_equal))
            v.tensor_tensor(v_sum[0:1, :], v_sum[0:1, :], f_b[0:1, 0:1], ALU.add).then_inc(s_viol, 1)
            v.tensor_copy(REC[:, 0:C, 0], e_s[:, :])
            v.tensor_copy(REC[:, 0:C, 1], e_d[:, :])
            link(v.tensor_tensor(f_a[:, :], e_prev[:, :], e_d[:, :], ALU.is_equal))
            link(v.tensor_scalar(f_a[:, :], f_a[:, :], float(FAR), None, ALU.mult))
            link(v.tensor_tensor(REC[:, 0:C, 2], f_a[:, :], e_d[:, :], ALU.add))
            link(v.tensor_scalar(f_nl[:, :], f_nl[:, :], float(-FAR), float(FAR), ALU.mult, ALU.add))
            link(v.tensor_tensor(f_a[:, :], e_no[:, :], e_d[:, :], ALU.subtract))
            link(v.tensor_tensor(REC[:, 0:C, 3], f_a[:, :], f_nl[:, :], ALU.add))
            v.tensor_copy(lane_no[:, :], IDX[:, 0, 0, 0:1]).then_inc(s_viol, 1)
            dve.wait_ge(s_viol, 2)
            for t in range(PAIR):
                link(v.tensor_scalar(slot_far[:, t:t + 1], lane_no[:, :], float(STRIDE), float(FAR),
                                     ALU.is_ge, ALU.mult))
            dve.wait_ge(s_flagp, 1)
            v.tensor_copy(flag[:, :], PT[0][0:1, 0:1]).then_inc(s_flag, 1)
            dve.wait_ge(s_small, 48)
            v.tensor_scalar(gcol[:, :], gcol[:, :], 0.5, None, ALU.mult)
            for k in range(KC):
                v.tensor_copy(bwide[:, k, :], wide(bcol[:, k:k + 1], LANES)).then_inc(s_half, 1)

            def low_parts(banks, hi, lo, hi_ready, done, n=0):
                for k, bank in enumerate(banks):
                    dve.wait_ge(hi_ready, n + k + 1)
                    v.scalar_tensor_tensor(out=lo[:, k, :], in0=bank[:, :], scalar=gcol[:, k:k + 1],
                                           in1=hi[:, k, :].bitcast(f32), op0=ALU.mult,
                                           op1=ALU.subtract).then_inc(done, 1)

            def weights():
                dve.wait_ge(s_half, KC)
                low_parts(W_BANKS[0], ws_hi, ws_lo, s_whi, s_wlo)
                low_parts(W_BANKS[1], wl_hi, wl_lo, s_whi, s_wlo, KC)

            def reciprocal(st, s, sd_ready, done):
                wait_alone(dve, sd_ready, s.times(1, 1))
                return v.reciprocal(st[3][:, s.slot(st[6]), :], st[2][:, s.slot(2), :]).then_inc(done, 1)

            def minus_mean(st, s, rs_done, done):
                dve.wait_ge(rs_done, s.times(1, 1))
                v.scalar_tensor_tensor(out=st[4][:, s.slot(st[6]), :], in0=st[1][:, s.slot(2), :, 0], scalar=-1.0,
                                       in1=st[3][:, s.slot(st[6]), :], op0=ALU.mult, op1=ALU.mult).then_inc(done, 1)

            def y_stats(s, t, y_done, bn_done):
                dve.wait_ge(y_done, s.times(PAIR, t + 1))
                v.bn_stats(ys[0][:, s.slot(2), t, :], Y[:, s.slot(2), t, :]).then_inc(bn_done, 1)

            def y_aggr(s, t, bn_done, var_done):
                wait_alone(dve, bn_done, s.times(PAIR, t + 1))
                v.bn_aggr(ys[1][:, s.slot(2), t, :], ys[0][:, s.slot(2), t, :]).then_inc(var_done, 1)

            def step_b(s):
                n, e = s.plus(3), s.plus(-1)
                slot = s.slot(2)

                def total(t):
                    dve.wait_ge(b_z, s.times(PAIR, t + 1))
                    if s.plus(-2).exists() and t == 0:
                        dve.wait_ge(b_ts[slot], s.turn(2, 16))
                    v.tensor_tensor(T[:, slot, t, 0:D], PZ[slot][t][:, :], bias_s[:, :], ALU.add).then_inc(b_t, 1)

                def rectified(t):
                    if s.plus(-2).exists():
                        dve.wait_ge(b_out, s.plus(-2).times(PAIR, t + 1))
                    dve.wait_ge(b_t, s.times(PAIR, t + 1))
                    v.scalar_tensor_tensor(out=Y[:, slot, t, :], in0=T[:, slot, t, 0:D], scalar=0.0,
                                           in1=X[:, s.slot(UNROLL), t, :], op0=ALU.max, op1=ALU.add).then_inc(b_y, 1)

                def x_stats(t):
                    if t == 0:
                        dve.wait_ge(b_ld[n.slot(UNROLL)], n.turn(UNROLL, 16, 16))
                        if s.plus(1).exists():
                            dve.wait_ge(b_zn, s.plus(1).times(PAIR, PAIR))
                    v.bn_stats(xs[0][:, n.slot(2), t, :], X[:, n.slot(UNROLL), t, :]).then_inc(b_bn, 1)

                if s.reg is None and s.at == -2:
                    weights()
                if s.reg is None and s.at == 0:
                    dve.wait_ge(s_bias, 1)
                    v.tensor_scalar(bias_s[:, :], PS[0][:, :], 0.5, None, ALU.mult).then_inc(s_bias, 1)
                    dve.wait_ge(s_bias, 2)
                if s.exists():
                    total(0)
                if e.exists():
                    reciprocal(ys, e, b_ysd, b_yrs)
                if s.exists():
                    v.tensor_scalar(T[:, slot, :, D:STATW], xs[5][:, s.slot(UNROLL), :, :], -1.0, None,
                                    ALU.mult)
                    rectified(0)
                if e.exists():
                    minus_mean(ys, e, b_yrs, b_ynm)
                if s.exists():
                    total(1)
                if n.exists():
                    x_stats(0)
                if s.exists():
                    rectified(1)
                if n.exists():
                    x_stats(1)
                if s.exists():
                    y_stats(s, 0, b_y, b_ybn)
                if n.exists():
                    for t in range(PAIR):
                        wait_alone(dve, b_bn, n.times(PAIR, t + 1))
                        v.bn_aggr(xs[1][:, n.slot(2), t, :], xs[0][:, n.slot(2), t, :]).then_inc(b_var, 1)
                if s.exists():
                    y_stats(s, 1, b_y, b_ybn)
                if n.exists():
                    reciprocal(xs, n, b_sd, b_rs)
                if s.exists():
                    y_aggr(s, 0, b_ybn, b_yvar)
                if n.exists():
                    minus_mean(xs, n, b_rs, b_nm)
                if s.exists():
                    y_aggr(s, 1, b_ybn, b_yvar)

            def step_a(s):
                e, m, n, g = s.plus(-1), s.plus(1), s.plus(2), s.plus(3)
                slot, q = s.slot(2), s.slot(UNROLL)

                def total(t):
                    if t == 0:
                        dve.wait_ge(a_gt[q], s.turn(UNROLL, 16 * PAIR, 16 * PAIR))
                        dve.wait_ge(a_rc, s.times(1, 1))
                    dve.wait_ge(a_z, s.times(PAIR, t + 1))
                    if s.plus(-2).exists():
                        dve.wait_ge(a_out, s.plus(-2).times(PAIR, t + 1))
                    v.scalar_tensor_tensor(out=Y[:, slot, t, :], in0=PZ[slot][t][:, :], scalar=RC[:, slot, t:t + 1],
                                           in1=T[:, q, t, 0:D], op0=ALU.mult, op1=ALU.add).then_inc(a_t1, 1)

                def rectified(t):
                    dve.wait_ge(a_t1, s.times(PAIR, t + 1))
                    v.scalar_tensor_tensor(out=Y[:, slot, t, :], in0=Y[:, slot, t, :], scalar=0.0,
                                           in1=X[:, q, t, :], op0=ALU.max, op1=ALU.add).then_inc(a_y, 1)

                def same_dst(t):
                    if s.exists():
                        dve.wait_ge(a_U, s.times(PAIR, PAIR))
                    dve.wait_ge(a_D, n.times(PAIR, t + 1))
                    v.tensor_scalar(SEL[:, n.slot(2), t, :], PT[t][:, 0:LANES], DCF[:, n.slot(UNROLL), t:t + 1],
                                    None, ALU.is_equal).then_inc(a_sel, 1)

                def indices():
                    r = g.slot(UNROLL)
                    dve.wait_ge(a_idx[r], g.turn(UNROLL, 16 * PAIR, 16 * PAIR))
                    v.tensor_copy(DCF[:, r, :], IDX[:, r, :, 1])
                    old = g.plus(-UNROLL)
                    if old.exists():
                        dve.wait_ge(a_st[old.slot(2)], old.turn(2, 16 * PAIR, 16 * PAIR))
                    v.tensor_tensor(NID[:, r, :], IDX[:, r, :, 2], slot_far[:, :], ALU.add).then_inc(a_prep, 1)

                def low_part(t):
                    dve.wait_ge(a_hi, m.times(PAIR, t + 1))
                    if e.exists():
                        dve.wait_ge(a_z, e.times(PAIR, t + 1))
                    v.tensor_tensor(XL[:, m.slot(2), t, :], PS[t][:, :], XH[:, m.slot(2), t, :].bitcast(f32),
                                    ALU.subtract).then_inc(a_lo, 1)

                def difference(t):
                    dve.wait_ge(a_zg, n.times(PAIR, t + 1))
                    dve.wait_ge(a_zx, n.times(PAIR, t + 1))
                    zg = ZG[:, n.slot(2), t, 0:DIFFS]
                    v.tensor_tensor(zg, zg, ZX[:, n.slot(2), t, 0:DIFFS], ALU.add).then_inc(a_diff, 1)

                def source_stats(t):
                    if t == 0:
                        dve.wait_ge(a_gg[g.slot(UNROLL)], g.turn(UNROLL, 16 * PAIR, 16 * PAIR))
                        if m.exists():
                            dve.wait_ge(a_zg, m.times(PAIR, PAIR))
                    v.bn_stats(gs[0][:, g.slot(2), t, :], G[:, g.slot(2), t, :]).then_inc(a_bn, 1)

                def source_aggr(t):
                    wait_alone(dve, a_bn, g.times(PAIR, t + 1))
                    v.bn_aggr(gs[1][:, g.slot(2), t, :], gs[0][:, g.slot(2), t, :]).then_inc(a_var, 1)

                if s.reg is None and s.at == 0:
                    dve.wait_ge(b_out, NG * PAIR)
                if s.exists():
                    total(0)
                if e.exists():
                    reciprocal(ys, e, a_ysd, a_yrs)
                if n.exists():
                    reciprocal(gs, n, a_sd, a_rs)
                if m.exists():
                    dve.wait_ge(a_cnt, m.times(1, 1))
                    v.tensor_scalar(CNT[:, m.slot(2), :], CNT[:, m.slot(2), :], 1.0, None, ALU.add).then_inc(a_cnt1, 1)
                if e.exists():
                    minus_mean(ys, e, a_yrs, a_ynm)
                if n.exists():
                    minus_mean(gs, n, a_rs, a_nm)
                    for t in range(PAIR):
                        same_dst(t)
                if g.exists():
                    indices()
                if s.exists():
                    rectified(0)
                if m.exists():
                    low_part(0)
                if s.exists():
                    total(1)
                if m.exists():
                    low_part(1)
                if s.exists():
                    rectified(1)
                if m.exists():
                    dve.wait_ge(a_cnt1, m.times(1, 1))
                    v.reciprocal(RC[:, m.slot(2), :], CNT[:, m.slot(2), :]).then_inc(a_rc, 1)
                if n.exists():
                    difference(PAIR - 1)
                if g.exists():
                    source_stats(0)
                if n.exists():
                    dve.wait_ge(a_sel, n.times(PAIR, PAIR))
                    v.reduce_sum(CNT[:, n.slot(2), :], SEL[:, n.slot(2), :, :], AX.X).then_inc(a_cnt, 1)
                if s.exists():
                    y_stats(s, 0, a_y, a_ybn)
                if g.exists():
                    source_stats(1)
                    source_aggr(0)
                if s.exists():
                    y_stats(s, 1, a_y, a_ybn)
                if g.exists():
                    source_aggr(1)
                if s.exists():
                    y_aggr(s, 0, a_ybn, a_yvar)
                if s.exists():
                    y_aggr(s, 1, a_ybn, a_yvar)

            def fast():
                run_steps(dve, NG, 5, 2, step_b)
                run_steps(dve, NA, 5, 2, step_a)

            def general():
                def count(at):
                    seen = [0]

                    def then(ins):
                        seen[0] += 1
                        ins.then_inc(g_dve, 1)
                        wait_alone(dve, g_dve, at(seen[0]))
                    return then, seen

                weights()
                low_parts(W_BANKS[0], wr_hi, wr_lo, g_whi, g_wlo)
                dve.wait_ge(g_bias, 1)
                v.tensor_scalar(bias_l[:, :], PS[0][:, :], 0.5, None, ALU.mult)
                v.tensor_scalar(bias_r[:, :], PL[0][:, :], 0.5, None, ALU.mult).then_inc(g_setup, 1)

                with dve.Fori(0, C) as k:
                    then, seen = count(lambda n: CHUNK_DVE(k, n))
                    dve.wait_ge(g_ld, k * 32 + 32)
                    then(v.tensor_copy(DCF[0:P, 0, 0:1], IDX[0:P, 0, 0, 1:2]))
                    then(v.tensor_copy(DB[0:P, 0, 0, 0:P], wide(IDX[0:P, 0, 0, 1:2], P)))
                    dve.wait_ge(g_gat, k * 16 + 16)
                    then(v.bn_stats(gs[0][0:P, 0, 0, :], G[0:P, 0, 0, :]))
                    then(v.bn_aggr(gs[1][0:P, 0, 0, :], gs[0][0:P, 0, 0, :]))
                    dve.wait_ge(g_act, CHUNK_ACT(k, 1))
                    then(v.reciprocal(gs[3][0:P, 0, 0:1], gs[2][0:P, 0, 0:1]))
                    then(v.scalar_tensor_tensor(out=gs[4][0:P, 0, 0:1], in0=gs[1][0:P, 0, 0, 0:1], scalar=-1.0,
                                                in1=gs[3][0:P, 0, 0:1], op0=ALU.mult, op1=ALU.mult))
                    dve.wait_ge(g_pe, CHUNK_PE(k, 1))
                    then(v.tensor_scalar(SEL[0:P, 0, 0, 0:P], PT[0][0:P, 0:P], DCF[0:P, 0, 0:1], None,
                                         ALU.is_equal))
                    then(v.reduce_sum(S2[0:P, D:D + 1], SEL[0:P, 0, 0, 0:P], AX.X))
                    then(v.tensor_tensor(SEL[0:P, 0, 1, 0:P], SEL[0:P, 0, 0, 0:P], earlier[0:P, 0:P], ALU.mult))
                    then(v.reduce_sum(CNT[0:P, 0, 0:1], SEL[0:P, 0, 1, 0:P], AX.X))
                    then(v.tensor_scalar(CNT[0:P, 0, 0:1], CNT[0:P, 0, 0:1], 0.0, None, ALU.is_gt))
                    then(v.tensor_scalar(RC[0:P, 0, 0:1], lane_no[0:P, :], float(N), None, ALU.add))
                    then(v.tensor_tensor(RC[0:P, 0, 0:1], RC[0:P, 0, 0:1], DCF[0:P, 0, 0:1], ALU.subtract))
                    then(v.tensor_tensor(RC[0:P, 0, 0:1], RC[0:P, 0, 0:1], CNT[0:P, 0, 0:1], ALU.mult))
                    then(v.tensor_tensor(NID[0:P, 0, 0:1], RC[0:P, 0, 0:1], DCF[0:P, 0, 0:1], ALU.add))
                    dve.wait_ge(g_pe, CHUNK_PE(k, 2))
                    then(v.tensor_copy(S2[0:P, 0:D], PL[0][0:P, :]))
                    then(v.memset(SEL[0:P, 0, 1, 0:P], 0.0))
                    assert seen[0] == EDGE_DVE

                def tile(i):
                    then, seen = count(lambda n: TILE_DVE(i, n))
                    dve.wait_ge(g_in, i * 32 + 32)
                    then(v.bn_stats(xs[0][:, 0, 0, :], X[:, 0, 0, :]))
                    then(v.bn_aggr(xs[1][:, 0, 0, :], xs[0][:, 0, 0, :]))
                    then(v.tensor_scalar(CNT[:, 0, 0:1], S2[:, D:D + 1], 1.0, None, ALU.max))
                    then(v.reciprocal(RC[:, 0, 0:1], CNT[:, 0, 0:1]))
                    then(v.tensor_scalar(CNT[:, 0, 1:2], S2[:, D:D + 1], 1.0, None, ALU.min))
                    then(v.tensor_scalar(ZG[:, 0, 0, :], S2[:, 0:D], RC[:, 0, 0:1], None, ALU.mult))
                    dve.wait_ge(g_act, TILE_ACT(i, 1))
                    then(v.reciprocal(xs[3][:, 0, 0:1], xs[2][:, 0, 0:1]))
                    then(v.scalar_tensor_tensor(out=xs[4][:, 0, 0:1], in0=xs[1][:, 0, 0, 0:1], scalar=-1.0,
                                                in1=xs[3][:, 0, 0:1], op0=ALU.mult, op1=ALU.mult))
                    dve.wait_ge(g_act, TILE_ACT(i, 3))
                    v.tensor_tensor(XL[:, 0, 0, :], PT[0][:, :], XH[:, 0, 0, :].bitcast(f32), ALU.subtract)
                    then(v.tensor_tensor(SL[:, :], PS[0][:, :], SH[:, :].bitcast(f32),
                                         ALU.subtract))
                    dve.wait_ge(g_pe, TILE_PE(i, 2))
                    then(v.tensor_tensor(Y[:, 0, 0, :], PL[0][:, :], bias_r[:, :], ALU.add))
                    then(v.scalar_tensor_tensor(out=Y[:, 0, 0, :], in0=bias_l[:, :], scalar=CNT[:, 0, 1:2],
                                                in1=Y[:, 0, 0, :], op0=ALU.mult, op1=ALU.add))
                    then(v.scalar_tensor_tensor(out=Y[:, 0, 0, :], in0=Y[:, 0, 0, :], scalar=0.0,
                                                in1=X[:, 0, 0, :], op0=ALU.max, op1=ALU.add))
                    then(v.bn_stats(ys[0][:, 0, 0, :], Y[:, 0, 0, :]))
                    then(v.bn_aggr(ys[1][:, 0, 0, :], ys[0][:, 0, 0, :]))
                    dve.wait_ge(g_act, TILE_ACT(i, 4))
                    then(v.reciprocal(ys[3][:, 0, 0:1], ys[2][:, 0, 0:1]))
                    then(v.scalar_tensor_tensor(out=ys[4][:, 0, 0:1], in0=ys[1][:, 0, 0, 0:1], scalar=-1.0,
                                                in1=ys[3][:, 0, 0:1], op0=ALU.mult, op1=ALU.mult))
                    assert seen[0] == T_DVE

                with dve.Fori(0, NT - 1) as i:
                    tile(i)
                tile(NT - 1)

            when_fast(dve, fast, general)

        @block.scalar
        def _(act):
            a = nc.scalar

            def raw_copies(banks, to, ready, n, done):
                for k, bank in enumerate(banks):
                    act.wait_ge(ready, n + k + 1)
                    a.activation(to[:, k // PAIR, k % PAIR, :], bank[:, :], ACT.Identity).then_inc(done, 1)

            def high_parts(banks, hi, ready, n, done):
                for k, bank in enumerate(banks):
                    act.wait_ge(ready, n + k + 1)
                    a.activation(hi[:, k, :], bank[:, :], ACT.Identity, scale=gcol[:, k:k + 1]).then_inc(done, 1)

            def weights():
                raw_copies(W_BANKS[0], Y, s_wT, 0, s_raw)
                act.wait_ge(s_half, KC)
                high_parts(W_BANKS[0], ws_hi, s_wT, 0, s_whi)
                high_parts(W_BANKS[1], wl_hi, s_wT, KC, s_whi)

            def sqrt(sd, mv, slot, eps, ready, value, done):
                act.wait_ge(ready, value)
                a.activation(sd[:, slot, :], mv[:, slot, :, 1], ACT.Sqrt, bias=eps[:, 0:1]).then_inc(done, 1)

            def normalized(to, rows, st, slot, t):
                return a.activation(to, rows, ACT.Identity, bias=st[4][:, slot, t:t + 1],
                                    scale=st[3][:, slot, t:t + 1])

            def step_b(s):
                if s.reg is None and s.at == -1:
                    weights()
                m = s.plus(1)
                if m.exists():
                    for t in range(PAIR):
                        act.wait_ge(b_T, m.times(PAIR, t + 1))
                        if s.plus(-1).exists():
                            act.wait_ge(b_z, s.plus(-1).times(PAIR, t + 1))
                        a.activation(XT[:, m.slot(2), t, :], PT[t][:, :], ACT.Identity)
                        a.activation(XH[:, m.slot(2), t, :], PT[t][:, :], ACT.Identity).then_inc(b_hi, 1)
                n, e, y = s.plus(2), s.plus(-1), s.plus(-2)
                if y.exists():
                    act.wait_ge(b_ynm, y.times(1, 1))
                    if y.plus(-2).exists():
                        act.wait_ge(b_st[y.slot(2)], y.turn(2, 16))
                    for t in range(PAIR):
                        normalized(O[:, y.slot(2), t, :], Y[:, y.slot(2), t, :], ys, y.slot(2), t).then_inc(b_out, 1)
                if n.exists():
                    sqrt(xs[2], xs[1], n.slot(2), eps1, b_var, n.times(PAIR, PAIR), b_sd)
                if e.exists():
                    sqrt(ys[2], ys[1], e.slot(2), eps4, b_yvar, e.times(PAIR, PAIR), b_ysd)
                if n.exists():
                    act.wait_ge(b_nm, n.times(1, 1))
                    if s.exists():
                        act.wait_ge(b_T, s.times(PAIR, PAIR))
                    for t in range(PAIR):
                        normalized(ZX[:, n.slot(2), t, :], X[:, n.slot(UNROLL), t, :], xs, n.slot(UNROLL),
                                   t).then_inc(b_zn, 1)

            def step_a(s):
                y, e, m, n = s.plus(-2), s.plus(-1), s.plus(1), s.plus(2)
                if y.exists():
                    act.wait_ge(a_ynm, y.times(1, 1))
                    if y.plus(-2).exists():
                        act.wait_ge(a_st[y.slot(2)], y.turn(2, 16 * PAIR))
                    elif y.at == 0:
                        all_stored(act, b_st)
                    for t in range(PAIR):
                        normalized(O[:, y.slot(2), t, :], Y[:, y.slot(2), t, :], ys, y.slot(2), t).then_inc(a_out, 1)
                if e.exists():
                    sqrt(ys[2], ys[1], e.slot(2), eps4, a_yvar, e.times(PAIR, PAIR), a_ysd)
                if n.exists():
                    sqrt(gs[2], gs[1], n.slot(2), eps1, a_var, n.times(PAIR, PAIR), a_sd)
                if m.exists():
                    for t in range(PAIR):
                        act.wait_ge(a_U, m.times(PAIR, t + 1))
                        if e.exists():
                            act.wait_ge(a_z, e.times(PAIR, t + 1))
                        a.activation(XH[:, m.slot(2), t, :], PS[t][:, :], ACT.Identity).then_inc(a_hi, 1)
                if n.exists():
                    q = n.slot(UNROLL)
                    if s.exists():
                        act.wait_ge(a_U, s.times(PAIR, PAIR))
                    act.wait_ge(a_nm, n.times(1, 1))
                    for t in range(PAIR):
                        normalized(ZG[:, n.slot(2), t, :], G[:, n.slot(2), t, :], gs, n.slot(2), t).then_inc(a_zg, 1)
                        if t == 0:
                            act.wait_ge(a_gx[q], n.turn(UNROLL, 16 * PAIR, 16 * PAIR))
                            act.wait_ge(a_gt[q], n.turn(UNROLL, 16 * PAIR, 16 * PAIR))
                        a.activation(ZX[:, n.slot(2), t, :], X[:, q, t, :], ACT.Identity, bias=T[:, q, t, D + 1:D + 2],
                                     scale=T[:, q, t, D:D + 1]).then_inc(a_zx, 1)
                w = s.plus(4)
                if w.exists():
                    r = w.slot(UNROLL)
                    act.wait_ge(a_idx[r], w.turn(UNROLL, 16 * PAIR, 16 * PAIR))
                    if w.plus(-2).exists():
                        act.wait_ge(a_D, w.plus(-2).times(PAIR, PAIR))
                    for t in range(PAIR):
                        a.activation(DB[:, w.slot(2), t, :], wide(IDX[:, r, t, 1:2], LANES),
                                     ACT.Identity).then_inc(a_wide, 1)

            def fast():
                run_steps(act, NG, 5, 2, step_b)
                act.wait_ge(b_z, NG * PAIR)
                run_steps(act, NA, 5, 2, step_a)

            def general():
                weights()
                raw_copies(W_BANKS[0], O, g_wT, 0, g_raw)
                high_parts(W_BANKS[0], wr_hi, g_wT, 0, g_whi)
                raw_copies(W_BANKS[1], Y, g_wT, KC, g_raw)
                with act.Fori(0, C) as k:
                    act.wait_ge(g_dve, CHUNK_DVE(k, 4))
                    a.activation(gs[2][0:P, 0, 0:1], gs[1][0:P, 0, 0, 1:2], ACT.Sqrt,
                                 bias=eps1[0:P, 0:1]).then_inc(g_act, 1)
                    act.wait_ge(g_dve, CHUNK_DVE(k, 6))
                    a.activation(ZG[0:P, 0, 0, :], G[0:P, 0, 0, :], ACT.Identity, bias=gs[4][0:P, 0, 0:1],
                                 scale=gs[3][0:P, 0, 0:1]).then_inc(g_act, 1)

                def tile(i):
                    act.wait_ge(g_dve, TILE_DVE(i, 2))
                    a.activation(xs[2][:, 0, 0:1], xs[1][:, 0, 0, 1:2], ACT.Sqrt, bias=eps1[:, 0:1]).then_inc(g_act, 1)
                    act.wait_ge(g_dve, TILE_DVE(i, 8))
                    normalized(ZX[:, 0, 0, :], X[:, 0, 0, :], xs, 0, 0).then_inc(g_act, 1)
                    act.wait_ge(g_pe, TILE_PE(i, 1))
                    a.activation(XH[:, 0, 0, :], PT[0][:, :], ACT.Identity)
                    a.activation(SH[:, :], PS[0][:, :], ACT.Identity).then_inc(g_act, 1)
                    act.wait_ge(g_dve, TILE_DVE(i, 14))
                    a.activation(ys[2][:, 0, 0:1], ys[1][:, 0, 0, 1:2], ACT.Sqrt, bias=eps4[:, 0:1]).then_inc(g_act, 1)
                    act.wait_ge(g_dve, TILE_DVE(i, 16))
                    normalized(O[:, 0, 0, :], Y[:, 0, 0, :], ys, 0, 0).then_inc(g_act, 1)

                with act.Fori(0, NT - 1) as i:
                    tile(i)
                tile(NT - 1)

            when_fast(act, fast, general)

        @block.tensor
        def _(pe):
            m_ = nc.tensor

            def chunk(b, k):
                return b[:, k * LANES:(k + 1) * LANES]

            def product(bank, hi, lo, w_hi, w_lo, wait_hi, wait_lo, start=True, stop=True):
                wait_hi()
                for k in range(KC):
                    m_.matmul(bank, chunk(hi, k), w_hi[:, k, :], start=start and k == 0, stop=False)
                    m_.matmul(bank, chunk(hi, k), w_lo[:, k, :], start=False, stop=False)
                wait_lo()
                for k in range(KC):
                    last = m_.matmul(bank, chunk(lo, k), w_hi[:, k, :], start=False, stop=stop and k == KC - 1)
                return last

            pe.wait_ge(s_const, 1)
            pe.wait_ge(s_viol, 1)
            m_.matmul(PT[0][0:1, 0:1], v_sum[:, :], ones[0:P, 0:1], start=True, stop=True).then_inc(s_flagp, 1)
            def bias_row(bank, raw, stop=False):
                for k in range(KC):
                    last = m_.matmul(bank, bwide[:, k, :], raw[:, k // PAIR, k % PAIR, :],
                                     start=k == 0, stop=stop and k == KC - 1)
                return last

            def weight(full, o, k):
                return chunk(full[:, o // PAIR, o % PAIR, :], k)

            pe.wait_ge(s_w, 32)
            for k, bank in enumerate(W_BANKS[0]):
                for o in range(KC):
                    m_.matmul(chunk(bank, o), weight(G, o, k), ident[:, :], start=True, stop=False)
                    last = m_.matmul(chunk(bank, o), weight(ZG, o, k), ident[:, :], start=False, stop=True)
                last.then_inc(s_wT, 1)
            pe.wait_ge(s_flag, 1)
            for k, bank in enumerate(W_BANKS[1]):
                for o in range(KC):
                    last = m_.transpose(chunk(bank, o), weight(G, o, k), ident[:, :])
                last.then_inc(s_wT, 1)
            def transposed(bank, rows):
                for k in range(KC):
                    last = m_.transpose(chunk(bank, k), chunk(rows, k), ident[:, :])
                return last

            def step_b(s):
                n = s.plus(1)
                if s.reg is None and s.at == -1:
                    pe.wait_ge(s_half, KC)
                    pe.wait_ge(s_raw, KC)
                    pe.wait_ge(s_wlo, 1)
                    bias_row(PS[0][:, :], Y)
                    m_.matmul(PS[0][:, :], ones[0:1, :], blrow[0:1, :], start=False, stop=True).then_inc(s_bias, 1)
                    pe.wait_ge(s_wlo, 2 * KC)
                if n.exists():
                    for t in range(PAIR):
                        pe.wait_ge(b_zn, n.times(PAIR, t + 1))
                        if s.exists():
                            pe.wait_ge(b_hi, s.times(PAIR, t + 1))
                        transposed(PT[t], ZX[:, n.slot(2), t, :]).then_inc(b_T, 1)
                if s.exists():
                    for t in range(PAIR):
                        if s.plus(-2).exists():
                            pe.wait_ge(b_t, s.plus(-2).times(PAIR, t + 1))
                        product(PZ[s.slot(2)][t][:, :], XH[:, s.slot(2), t, :], XL[:, s.slot(2), t, :], ws_hi, ws_lo,
                                lambda: pe.wait_ge(b_hi, s.times(PAIR, t + 1)),
                                lambda: pe.wait_ge(b_lo, s.times(PAIR, t + 1))).then_inc(b_z, 1)

            def step_a(s):
                m, n, g = s.plus(1), s.plus(2), s.plus(3)
                for t in range(PAIR):
                    if m.exists():
                        pe.wait_ge(a_sel, m.times(PAIR, t + 1))
                        if s.exists():
                            pe.wait_ge(a_lo, s.times(PAIR, t + 1))
                        pe.wait_ge(a_zg, m.times(PAIR, t + 1))
                        pe.wait_ge(a_zx, m.times(PAIR, t + 1))
                        if t == PAIR - 1:
                            pe.wait_ge(a_diff, m.times(1, 1))
                        for k in range(KC):
                            parts = (ZG,) if t == PAIR - 1 and k * LANES < DIFFS else (ZG, ZX)
                            for z in parts:
                                last = m_.matmul(chunk(PS[t], k), chunk(z[:, m.slot(2), t, :], k),
                                                 SEL[:, m.slot(2), t, :], start=z is parts[0], stop=z is parts[-1])
                        last.then_inc(a_U, 1)
                    if s.exists():
                        if s.plus(-2).exists():
                            pe.wait_ge(a_t1, s.plus(-2).times(PAIR, t + 1))
                        product(PZ[s.slot(2)][t][:, :], XH[:, s.slot(2), t, :], XL[:, s.slot(2), t, :], wl_hi, wl_lo,
                                lambda: pe.wait_ge(a_hi, s.times(PAIR, t + 1)),
                                lambda: pe.wait_ge(a_lo, s.times(PAIR, t + 1))).then_inc(a_z, 1)
                if g.exists():
                    for t in range(PAIR):
                        pe.wait_ge(a_wide, g.times(PAIR, t + 1))
                        if n.exists():
                            pe.wait_ge(a_sel, n.times(PAIR, t + 1))
                        m_.transpose(PT[t][:, 0:LANES], DB[:, g.slot(2), t, :], ident[:, :]).then_inc(a_D, 1)

            def fast():
                run_steps(pe, NG, 5, 2, step_b)
                pe.wait_ge(b_hi, NG * PAIR)
                pe.wait_ge(b_t, NG * PAIR)
                run_steps(pe, NA, 5, 2, step_a)

            def general():
                pe.wait_ge(s_wlo, 2 * KC)
                pe.wait_ge(s_half, KC)
                for banks, full in ((W_BANKS[0], ZG), (W_BANKS[1], G)):
                    for k, bank in enumerate(banks):
                        for o in range(KC):
                            last = m_.transpose(chunk(bank, o), weight(full, o, k), ident[:, :])
                        last.then_inc(g_wT, 1)
                pe.wait_ge(g_raw, 2 * KC)
                pe.wait_ge(g_wlo, KC)
                bias_row(PL[0][:, :], O)
                m_.matmul(PL[0][:, :], ones[0:1, :], blrow[0:1, :], start=False, stop=True)
                bias_row(PS[0][:, :], Y, stop=True).then_inc(g_bias, 1)
                pe.wait_ge(g_setup, 1)
                with pe.Fori(0, C) as k:
                    pe.wait_ge(g_dve, CHUNK_DVE(k, 2))
                    m_.matmul(PT[0][0:P, 0:P], DB[0:P, 0, 0, 0:P], ident[0:P, 0:P],
                              start=True, stop=True).then_inc(g_pe, 1)
                    pe.wait_ge(g_dve, CHUNK_DVE(k, 7))
                    pe.wait_ge(g_act, CHUNK_ACT(k, 2))
                    m_.matmul(PL[0][0:P, :], SEL[0:P, 0, 0, 0:P], ZG[0:P, 0, 0, :],
                              start=True, stop=True).then_inc(g_pe, 1)

                def tile(i):
                    pe.wait_ge(g_dve, TILE_DVE(i, 8))
                    pe.wait_ge(g_act, TILE_ACT(i, 2))
                    transposed(PT[0], ZX[:, 0, 0, :])
                    transposed(PS[0], ZG[:, 0, 0, :]).then_inc(g_pe, 1)
                    pe.wait_ge(g_dve, TILE_DVE(i, 9))
                    ready = lambda: None
                    product(PL[0][:, :], XH[:, 0, 0, :], XL[:, 0, 0, :], wr_hi, wr_lo, ready, ready, stop=False)
                    product(PL[0][:, :], SH[:, :], SL[:, :], wl_hi, wl_lo, ready, ready,
                            start=False).then_inc(g_pe, 1)

                with pe.Fori(0, NT - 1) as i:
                    tile(i)
                tile(NT - 1)

            when_fast(pe, fast, general)


_INS = ["x", "src", "dst", "L0_gnn_W_l", "L0_gnn_b_l", "L0_gnn_W_r", "L0_gnn_gamma", "L0_gnn_beta"]


def kernel(**inputs):
    import numpy as _np
    import concourse.bacc as _bacc
    from concourse import mybir as _mybir
    from concourse.bass_utils import run_bass_kernel_spmd as _run

    nc = _bacc.Bacc("TRN2", target_bir_lowering=False, num_devices=1)
    arrays, args = {}, []
    for name in _INS:
        a = _np.ascontiguousarray(inputs[name])
        arrays[f"in_{name}"] = a
        args.append(nc.dram_tensor(f"in_{name}", a.shape, _mybir.dt.from_np(a.dtype), kind="ExternalInput").ap())
    shape = arrays["in_x"].shape
    result = nc.dram_tensor("result", shape, _mybir.dt.float32, kind="ExternalOutput").ap()
    gnn_kernel(nc, *args, result)
    r = _run(nc, [arrays], core_ids=[0])
    return r.results[0]["result"]
```
